# Optimizing a Trainium2 kernel written in Bass

```python
import numpy as np
import jax
import jax.numpy as jnp

def _softmax(x, axis=-1):
    return jax.nn.softmax(x, axis=axis)

def _gelu(x):
    return jax.nn.gelu(x, approximate=True)

def _silu(x):
    return jax.nn.silu(x)

def _sigmoid(x):
    return jax.nn.sigmoid(x)

def _layernorm(x, axis=-1, eps=1e-05):
    m = jnp.mean(x, axis=axis, keepdims=True)
    v = jnp.var(x, axis=axis, keepdims=True)
    return (x - m) / jnp.sqrt(v + eps)

def _scatter_add(tgt, idx, src, axis=0):
    return tgt.at[idx].add(src)

def _segment_sum(src, seg, n):
    return jax.ops.segment_sum(src, seg, n)
kernel_name = 'mk_adaln_d1_jaxref_r8_cfa9b4'

def setup_inputs(seed: int=0):
    np.random.seed(seed)
    _w = jnp.asarray

    def _L0_attn_setup():
        import jax, jax.numpy as jnp
        import numpy as np
        import math
        B, L, H, D, HID = (2, 128, 16, 64, 128)

        def _rope_tables(seq_len, dim):
            inv_freq = 1.0 / 10000.0 ** (jnp.arange(0, dim, 2, dtype=jnp.float32) / dim)
            t = jnp.arange(seq_len, dtype=jnp.float32)
            freqs = jnp.outer(t, inv_freq)
            emb = jnp.concatenate([freqs, freqs], -1)
            return (jnp.cos(emb), jnp.sin(emb))

        def _rotate_half(x):
            x1, x2 = jnp.split(x, 2, axis=-1)
            return jnp.concatenate([-x2, x1], axis=-1)

        def _apply_rope(x, cos, sin):
            return x * cos + _rotate_half(x) * sin

        def _forward(x, w_qkv, w_o, log_p, log_a, w1, b1, w2, b2):
            Bx, Lx, _ = x.shape
            qkv = jnp.dot(x, w_qkv).reshape(Bx, Lx, 3, H, D)
            qkv = jnp.transpose(qkv, (2, 0, 3, 1, 4))
            q, k, v = (qkv[0], qkv[1], qkv[2])
            cos, sin = _rope_tables(Lx, D)
            cos, sin = (cos[None, None], sin[None, None])
            q = _apply_rope(q, cos, sin)
            k = _apply_rope(k, cos, sin)
            scale = 1.0 / math.sqrt(D)
            scores = jnp.einsum('bhid,bhjd->bhij', q, k) * scale
            pos = jnp.arange(Lx, dtype=jnp.float32)
            dist = jnp.abs(pos[None, :] - pos[:, None])
            p = jax.nn.softplus(log_p)
            a = jax.nn.softplus(log_a)
            kerple = -p * jnp.log1p(a * dist[None])
            attn_t = jnp.transpose(scores, (0, 2, 3, 1))
            kerple_t = jnp.broadcast_to(jnp.transpose(kerple, (1, 2, 0))[None], attn_t.shape)
            combined = jnp.concatenate([attn_t, kerple_t], axis=-1)
            hdn = jax.nn.gelu(jnp.dot(combined, w1) + b1, approximate=False)
            refined = jnp.dot(hdn, w2) + b2
            refined = jnp.transpose(refined, (0, 3, 1, 2))
            scores = scores + kerple[None] + refined
            causal = jnp.tril(jnp.ones((Lx, Lx), dtype=bool))
            scores = jnp.where(causal[None, None], scores, -jnp.inf)
            weights = jax.nn.softmax(scores, axis=-1)
            out = jnp.einsum('bhij,bhjd->bhid', weights, v)
            out = jnp.transpose(out, (0, 2, 1, 3)).reshape(Bx, Lx, H * D)
            return jnp.dot(out, w_o)
        key = jax.random.key(seed)
        ks = jax.random.split(key, 8)
        s = 0.02
        return {'x': jax.random.normal(ks[0], (B, L, HID), jnp.float32), 'w_qkv': jax.random.normal(ks[1], (HID, 3 * H * D), jnp.float32) * s, 'w_o': jax.random.normal(ks[2], (H * D, HID), jnp.float32) * s, 'log_p': jax.random.normal(ks[3], (H, 1, 1), jnp.float32) * 0.02, 'log_a': jax.random.normal(ks[4], (H, 1, 1), jnp.float32) * 0.02, 'w1': jax.random.normal(ks[5], (2 * H, 2 * H), jnp.float32) * s, 'b1': jnp.zeros((2 * H,), jnp.float32), 'w2': jax.random.normal(ks[6], (2 * H, H), jnp.float32) * s, 'b2': jnp.zeros((H,), jnp.float32)}
    _L0_attn_in = _L0_attn_setup()

    def _L0_ffn_setup():
        import jax, jax.numpy as jnp
        import numpy as np
        H = 128
        I = 64
        E = 8
        K = 2
        SI = I * 2
        B, S = (2, 128)

        def _mlp(x, gw, uw, dw):
            return jax.nn.silu(x @ gw.T) * (x @ uw.T) @ dw.T
        key = jax.random.key(seed)
        ks = jax.random.split(key, 9)
        s = 0.02
        return {'x': jax.random.normal(ks[0], (B, S, H), jnp.float32), 'gate_w': jax.random.normal(ks[1], (E, H), jnp.float32) * s, 'lb_bias': jnp.zeros((E,), jnp.float32), 'expert_gate_w': jax.random.normal(ks[2], (E, I, H), jnp.float32) * s, 'expert_up_w': jax.random.normal(ks[3], (E, I, H), jnp.float32) * s, 'expert_down_w': jax.random.normal(ks[4], (E, H, I), jnp.float32) * s, 'shared_gate_w': jax.random.normal(ks[5], (SI, H), jnp.float32) * s, 'shared_up_w': jax.random.normal(ks[6], (SI, H), jnp.float32) * s, 'shared_down_w': jax.random.normal(ks[7], (H, SI), jnp.float32) * s}
    _L0_ffn_in = _L0_ffn_setup()
    _L0_c = _w((lambda *s: np.random.randn(*s).astype(np.float32) * 0.05)(16, 128))
    _L0_wmod = _w((lambda *s: np.random.randn(*s).astype(np.float32) * 0.05)(128, 6 * 128) * 128 ** (-0.5))
    _d = {'L0_attn_x': _L0_attn_in['x'], 'L0_attn_w_qkv': _L0_attn_in['w_qkv'], 'L0_attn_w_o': _L0_attn_in['w_o'], 'L0_attn_log_p': _L0_attn_in['log_p'], 'L0_attn_log_a': _L0_attn_in['log_a'], 'L0_attn_w1': _L0_attn_in['w1'], 'L0_attn_b1': _L0_attn_in['b1'], 'L0_attn_w2': _L0_attn_in['w2'], 'L0_attn_b2': _L0_attn_in['b2'], 'L0_ffn_gate_w': _L0_ffn_in['gate_w'], 'L0_ffn_lb_bias': _L0_ffn_in['lb_bias'], 'L0_ffn_expert_gate_w': _L0_ffn_in['expert_gate_w'], 'L0_ffn_expert_up_w': _L0_ffn_in['expert_up_w'], 'L0_ffn_expert_down_w': _L0_ffn_in['expert_down_w'], 'L0_ffn_shared_gate_w': _L0_ffn_in['shared_gate_w'], 'L0_ffn_shared_up_w': _L0_ffn_in['shared_up_w'], 'L0_ffn_shared_down_w': _L0_ffn_in['shared_down_w'], 'L0_c': _L0_c, 'L0_wmod': _L0_wmod}
    _x0 = _d['L0_attn_x']
    _d['L0_attn_x'] = jax.random.normal(jax.random.fold_in(jax.random.key(seed), 1), (16, 256, 128), dtype=_x0.dtype)
    del _x0
    return _d

def reference(L0_attn_x, L0_attn_w_qkv, L0_attn_w_o, L0_attn_log_p, L0_attn_log_a, L0_attn_w1, L0_attn_b1, L0_attn_w2, L0_attn_b2, L0_ffn_gate_w, L0_ffn_lb_bias, L0_ffn_expert_gate_w, L0_ffn_expert_up_w, L0_ffn_expert_down_w, L0_ffn_shared_gate_w, L0_ffn_shared_up_w, L0_ffn_shared_down_w, L0_c, L0_wmod):

    def _L0_attn_ref(x, w_qkv, w_o, log_p, log_a, w1, b1, w2, b2):
        import jax, jax.numpy as jnp
        import numpy as np
        import math
        B, L, H, D, HID = (2, 128, 16, 64, 128)

        def _rope_tables(seq_len, dim):
            inv_freq = 1.0 / 10000.0 ** (jnp.arange(0, dim, 2, dtype=jnp.float32) / dim)
            t = jnp.arange(seq_len, dtype=jnp.float32)
            freqs = jnp.outer(t, inv_freq)
            emb = jnp.concatenate([freqs, freqs], -1)
            return (jnp.cos(emb), jnp.sin(emb))

        def _rotate_half(x):
            x1, x2 = jnp.split(x, 2, axis=-1)
            return jnp.concatenate([-x2, x1], axis=-1)

        def _apply_rope(x, cos, sin):
            return x * cos + _rotate_half(x) * sin

        def _forward(x, w_qkv, w_o, log_p, log_a, w1, b1, w2, b2):
            Bx, Lx, _ = x.shape
            qkv = jnp.dot(x, w_qkv).reshape(Bx, Lx, 3, H, D)
            qkv = jnp.transpose(qkv, (2, 0, 3, 1, 4))
            q, k, v = (qkv[0], qkv[1], qkv[2])
            cos, sin = _rope_tables(Lx, D)
            cos, sin = (cos[None, None], sin[None, None])
            q = _apply_rope(q, cos, sin)
            k = _apply_rope(k, cos, sin)
            scale = 1.0 / math.sqrt(D)
            scores = jnp.einsum('bhid,bhjd->bhij', q, k) * scale
            pos = jnp.arange(Lx, dtype=jnp.float32)
            dist = jnp.abs(pos[None, :] - pos[:, None])
            p = jax.nn.softplus(log_p)
            a = jax.nn.softplus(log_a)
            kerple = -p * jnp.log1p(a * dist[None])
            attn_t = jnp.transpose(scores, (0, 2, 3, 1))
            kerple_t = jnp.broadcast_to(jnp.transpose(kerple, (1, 2, 0))[None], attn_t.shape)
            combined = jnp.concatenate([attn_t, kerple_t], axis=-1)
            hdn = jax.nn.gelu(jnp.dot(combined, w1) + b1, approximate=False)
            refined = jnp.dot(hdn, w2) + b2
            refined = jnp.transpose(refined, (0, 3, 1, 2))
            scores = scores + kerple[None] + refined
            causal = jnp.tril(jnp.ones((Lx, Lx), dtype=bool))
            scores = jnp.where(causal[None, None], scores, -jnp.inf)
            weights = jax.nn.softmax(scores, axis=-1)
            out = jnp.einsum('bhij,bhjd->bhid', weights, v)
            out = jnp.transpose(out, (0, 2, 1, 3)).reshape(Bx, Lx, H * D)
            return jnp.dot(out, w_o)
        return _forward(x, w_qkv, w_o, log_p, log_a, w1, b1, w2, b2)

    def _L0_ffn_ref(x, gate_w, lb_bias, expert_gate_w, expert_up_w, expert_down_w, shared_gate_w, shared_up_w, shared_down_w):
        import jax, jax.numpy as jnp
        import numpy as np
        H = 128
        I = 64
        E = 8
        K = 2
        SI = I * 2
        B, S = (2, 128)

        def _mlp(x, gw, uw, dw):
            return jax.nn.silu(x @ gw.T) * (x @ uw.T) @ dw.T
        b, s, h = x.shape
        xf = x.reshape(-1, h)
        logits = xf @ gate_w.T + lb_bias
        scores = jax.nn.sigmoid(logits.astype(jnp.float32))
        topw, topi = jax.lax.top_k(scores, K)
        topw = (topw / (topw.sum(-1, keepdims=True) + 1e-08)).astype(x.dtype)
        out = jnp.zeros_like(xf)
        for e in range(E):
            m = topi == e
            sel = m.any(axis=-1)
            cnt = m.sum()
            wmean = (topw * m).sum() / jnp.maximum(cnt, 1).astype(topw.dtype)
            y = _mlp(xf, expert_gate_w[e], expert_up_w[e], expert_down_w[e])
            out = out + jnp.where(sel[:, None], y * wmean, jnp.zeros((), x.dtype))
        out = out.reshape(b, s, h)
        out = out + _mlp(x, shared_gate_w, shared_up_w, shared_down_w)
        return out
    x = L0_attn_x
    mod = (_silu(L0_c) @ L0_wmod).reshape(L0_c.shape[0], 6, 1, -1)
    sa, ca, ga, sb, cb, gb = (mod[:, 0], mod[:, 1], mod[:, 2], mod[:, 3], mod[:, 4], mod[:, 5])
    ga = (2 * (ga >= 0) - 1) * jnp.maximum(jnp.abs(ga), 0.25)
    gb = (2 * (gb >= 0) - 1) * jnp.maximum(jnp.abs(gb), 0.25)
    h = _layernorm(x, axis=-1) * (1 + ca) + sa
    x = x + ga * _L0_attn_ref(h, L0_attn_w_qkv, L0_attn_w_o, L0_attn_log_p, L0_attn_log_a, L0_attn_w1, L0_attn_b1, L0_attn_w2, L0_attn_b2)
    h = _layernorm(x, axis=-1) * (1 + cb) + sb
    x = x + gb * _L0_ffn_ref(h, L0_ffn_gate_w, L0_ffn_lb_bias, L0_ffn_expert_gate_w, L0_ffn_expert_up_w, L0_ffn_expert_down_w, L0_ffn_shared_gate_w, L0_ffn_shared_up_w, L0_ffn_shared_down_w)
    return x

_drawn_inputs = setup_inputs


def setup_inputs(seed=0):
    import zlib

    import numpy as np

    out = dict(_drawn_inputs(seed))
    spreads = {'L0_attn_b1': (0.0, 0.8), 'L0_attn_b2': (0.0, 0.8), 'L0_ffn_lb_bias': (0.0, 0.8)}
    factors = {'L0_attn_w_qkv': 8.0,
     'L0_attn_w_o': 8.0,
     'L0_attn_log_p': 8.0,
     'L0_attn_log_a': 8.0,
     'L0_attn_w1': 8.0,
     'L0_attn_w2': 8.0,
     'L0_ffn_gate_w': 8.0,
     'L0_ffn_expert_gate_w': 8.0,
     'L0_ffn_expert_up_w': 8.0,
     'L0_ffn_expert_down_w': 8.0,
     'L0_ffn_shared_gate_w': 8.0,
     'L0_ffn_shared_up_w': 8.0,
     'L0_ffn_shared_down_w': 8.0,
     'L0_c': 8.0,
     'L0_wmod': 8.0}
    for name, (base, spread) in spreads.items():
        noise = np.random.default_rng([zlib.crc32(name.encode()), seed]).standard_normal(out[name].shape)
        drawn = base * np.exp(spread * noise) if base else spread * noise
        out[name] = jnp.asarray(drawn.astype(out[name].dtype))
    for name, factor in factors.items():
        out[name] = (out[name] * factor).astype(out[name].dtype)
    return out
```

```python
import numpy as np
import concourse.bass as bass
from concourse import mybir
from contextlib import ExitStack

B, L, HID, H, D = 16, 256, 128, 16, 64
TT = L // 128
NT = B * TT
NPAIR = H // 2
E, I, TOPK = 8, 64, 2
HC = 2 * H
RI = 4
RP = 2 * RI
NP = L // RP
NB = 8
PPB = NP // NB
W = [32 * (k + 1) for k in range(NB)]
LEAD = RP * (PPB - 1)
SLACK = RP
SLOT = [w + SLACK for w in W]
CHUNKS = []
for k in range(NB):
    n = max(1, min(PPB, L // W[k]))
    for a in range(0, PPB, n):
        CHUNKS.append((k, a, n, W[k] if n > 1 else RP * (PPB * k + a + 1)))
NCH = len(CHUNKS)
NGRP = NP // 4 + NP // 8
SCALE = D ** -0.5
EPS_LN, EPS_TOP, FAR = 1e-5, 1e-8, -1e30
ROUTER_STEPS = 25


def row_pair_keys(p):
    return RP * (p + 1)


def shape_constants():
    f = np.float32
    inv = (f(1.0) / f(10000.0) ** (np.arange(0, D, 2, dtype=f) / f(D))).astype(f)
    ang = np.outer(np.arange(L, dtype=f), inv).astype(f)
    emb = np.concatenate([ang, ang], 1)
    cos, sin = np.cos(emb).T.astype(f), np.sin(emb).T.astype(f)
    sin[: D // 2] *= -1
    rope = np.concatenate([np.tile(cos, (2, 1)), np.tile(sin, (2, 1))], 1).astype(f)
    row = (np.arange(128) // 64) * RI + (np.arange(128) % 64) // H
    t = np.arange(L)
    future = np.where(t[None, :] - (L - RP) > row[:, None], f(FAR), f(0)).astype(f)
    tt = np.arange(L + SLACK)
    r = np.arange(64) // H
    dist = np.stack([np.abs(r[:, None] + RI * par - (tt[None, :] - (L - RP))) for par in range(2)], 1)
    pick = np.zeros((E, E // 2, 128), f)
    for m in range(E // 2):
        pick[2 * m, m, :64] = 1
        pick[2 * m + 1, m, 64:] = 1
    return {
        "k_ident": np.eye(128, dtype=f), "k_rope": rope,
        "k_future": future, "k_dist": dist.reshape(64, -1).astype(f), "k_pick": pick.reshape(E, -1),
        "k_rank": np.tile(E - np.arange(E, dtype=f), (128, NT)).astype(f),
    }


def build(nc, a, out):
    f32, bf16 = mybir.dt.float32, mybir.dt.bfloat16
    ALU, ACT, AX = mybir.AluOpType, mybir.ActivationFunctionType, mybir.AxisListType
    ds = bass.ds
    ctx = ExitStack()

    def sb(name, shape, dt=f32):
        return ctx.enter_context(nc.sbuf_tensor(name, shape, dt))

    def sem(name):
        return ctx.enter_context(nc.semaphore(name))

    def wait(eng, s, v):
        if not (isinstance(v, int) and v <= 0):
            eng.wait_ge(s, v)

    with ctx:
        ident = sb("ident", [128, 128])
        rope = sb("rope", [128, 2 * L])
        futb2 = sb("futb2", [128, L])
        wqkv = sb("wqkv", [128, 3 * H * D])
        wo = sb("wo", [128, NPAIR, HID])
        w1d, w2d = sb("w1d", [128, 128]), sb("w2d", [128, 64])
        selx = sb("selx", [128, 64])
        b1c, b2c, pac = sb("b1c", [128, 1]), sb("b2c", [128, 1]), sb("pac", [128, 12])
        wmod, cT = sb("wmod", [128, 6 * HID]), sb("cT", [128, 4, B])
        modc = sb("modc", [128, 4, B])
        cbc = sb("cbc", [128, 2, 128])
        gates = sb("gates", [128, B, HID])
        xall = sb("xall", [128, NT, HID])
        hT = sb("hT", [128, B * L])
        stat, mean = sb("stat", [128, NT, 6]), sb("mean", [128, NT])
        rstd, half = sb("rstd", [128, NT]), sb("half", [128, NT])
        xn = sb("xn", [128, 2, TT, HID])
        hcur = sb("hcur", [128, L])
        qT, kz = sb("qT", [128, 2, L]), sb("kz", [128, 2, 2, L])
        tmp = sb("tmp", [128, 2, 2 * L])
        V = sb("V", [128, TT, H * D])
        S0, S1 = sb("S0", [128, H, 128]), sb("S1", [128, H, L])
        X = [sb(f"X{k}", [128, 2 * PPB * SLOT[k]]) for k in range(NB)]
        Hs = sb("Hs", [128, 2, 512])
        P0, P1 = sb("P0", [128, NP // 2, 128]), sb("P1", [128, NP // 2, L])
        mx, rs, rr = sb("mx", [128, NP]), sb("rs", [128, NP]), sb("rr", [128, NP])
        PT0, PT1 = sb("PT0", [128, H, L]), sb("PT1", [128, H, 128])
        OT = sb("OT", [128, 4, L])
        yt = sb("yt", [128, TT, HID])

        PT0f = PT0[:, :, :].rearrange("p a b -> p (a b)")
        PT1f = PT1[:, :, :].rearrange("p a b -> p (a b)")
        S1f = S1[:, :, :].rearrange("p a b -> p (a b)")
        S0f = S0[:, :, :].rearrange("p a b -> p (a b)")
        eg = PT0f[:, 0:E * I]
        eu = PT0f[:, 512:512 + E * I]
        sg, su = PT0f[:, 1024:1152], PT0f[:, 1152:1280]
        dn = PT0f[:, 1280:1920].rearrange("p (m n) -> p m n", n=HID)
        gwT = PT0f[:, 1920:1928]
        lbb = PT0f[:, 2048:2048 + NT * E]
        rank = PT0f[:, 2304:2304 + NT * E]
        rt = PT1f.rearrange("p (k n) -> p k n", n=NT * E)
        lgT = V[0:E, 0, 0:1024].rearrange("p (k n) -> p k n", n=512)
        Vb = V[:, 1, :].bitcast(bf16)
        maskb, mcur, mT = Vb[:, 0:NT * E], Vb[:, 256:256 + 4 * E], Vb[0:E, 512:1024]
        pickb, identb = Vb[0:E, 1024:1536], Vb[:, 1536:1664]
        acts = S1f[:, 0:5 * 512].rearrange("p (m n) -> p m n", n=512)
        sil = S0f[:, 0:1024].rearrange("p (m n) -> p m n", n=512)
        res = S0f[:, 1024:2048].rearrange("p (m n) -> p m n", n=512)
        ones = sb("ones", [128, 128])
        top1, top2 = sb("top1", [128, NT]), sb("top2", [128, NT])
        tot, wm = sb("tot", [128, 4 * E]), sb("wm", [128, 4])

        bank = [ctx.enter_context(nc.psum_tensor(f"bank{n}", [128, 512], f32)) for n in range(8)]

        s_in = [sem(f"s_in{n}") for n in range(4)]
        s_zero = sem("s_zero")
        s_w12 = sem("s_w12")
        s_act0, s_dve0, s_pe0 = sem("s_act0"), sem("s_dve0"), sem("s_pe0")
        s_cb, s_gt, s_gd = sem("s_cb"), sem("s_gt"), sem("s_gd")
        s_st, s_bn, s_pw, s_xn = sem("s_st"), sem("s_bn"), sem("s_pw"), sem("s_xn")
        s_tr, s_ht = sem("s_tr"), sem("s_ht")
        s_hc = sem("s_hc")
        s_qk, s_rm, s_ra = sem("s_qk"), sem("s_rm"), sem("s_ra")
        s_sc, s_s0, s_s1 = sem("s_sc"), sem("s_s0"), sem("s_s1")
        s_x = [sem(f"s_rows{k}") for k in range(NB)]
        s_vp, s_v = sem("s_vp"), sem("s_v")
        s_h, s_g, s_l, s_m = sem("s_h"), sem("s_g"), sem("s_l"), sem("s_m")
        s_nm, s_e, s_rc, s_n = sem("s_nm"), sem("s_e"), sem("s_rc"), sem("s_n")
        s_t, s_td, s_ta = sem("s_t"), sem("s_td"), sem("s_ta")
        s_pv, s_o, s_yp, s_y, s_x1 = sem("s_pv"), sem("s_o"), sem("s_yp"), sem("s_y"), sem("s_x1")
        s_seen = sem("s_seen")
        s_inm = sem("s_inm")
        s_lp, s_lc, s_lt, s_dr = sem("s_lp"), sem("s_lc"), sem("s_lt"), sem("s_dr")
        s_al, s_tp, s_wm = sem("s_al"), sem("s_tp"), sem("s_wm")
        s_mc, s_mtp, s_mt, s_mb = sem("s_mc"), sem("s_mtp"), sem("s_mt"), sem("s_mb")
        s_gp, s_up, s_si, s_a1, s_a2 = sem("s_gp"), sem("s_up"), sem("s_si"), sem("s_a1"), sem("s_a2")
        s_dp, s_r1, s_r2, s_out = sem("s_dp"), sem("s_r1"), sem("s_r2"), sem("s_out")

        def p_slot(p):
            return P0[:, p, :] if p < NP // 2 else P1[:, p - NP // 2, :]

        def x_rows(k, par, a, n, w):
            v = X[k][:, par * PPB * SLOT[k]:(par + 1) * PPB * SLOT[k]].rearrange("q (m t) -> q m t", m=PPB)
            return v[:, a:a + n, W[k] - w:W[k]]

        block = ctx.enter_context(nc.Block())
        CPB = [[c for c in range(NCH) if CHUNKS[c][0] == k] for k in range(NB)]
        NPROJ, NSC = 2 * NPAIR, 2 * NPAIR

        @block.sync
        def _(sp):
            sp.dma_start(ident[:, :], a["k_ident"]).then_inc(s_in[0], 16)
            sp.dma_start(cT[:, 0, :], a["cT"]).then_inc(s_in[0], 16)
            sp.dma_start(wmod[:, :], a["wmod"]).then_inc(s_in[0], 16)
            sp.dma_start(pac[:, 0:2], a["pa"]).then_inc(s_in[0], 16)
            sp.dma_start(P1[64:128, 0:3, :].rearrange("p a b -> p (a b)")[:, 0:2 * (L + SLACK)], a["k_dist"]).then_inc(s_in[0], 16)
            sp.dma_start(xall[:, :, :], a["x"].rearrange("(t p) n -> p t n", p=128)).then_inc(s_in[1], 16)
            sp.dma_start(wqkv[:, :], a["wqkv"]).then_inc(s_in[2], 16)
            sp.dma_start(rope[:, :], a["k_rope"]).then_inc(s_in[2], 16)
            sp.dma_start(futb2[:, :], a["k_future"]).then_inc(s_in[3], 16)
            sp.dma_start(b1c[:, :], a["b1"]).then_inc(s_in[3], 16)
            sp.dma_start(b2c[:, :], a["b2"]).then_inc(s_in[3], 16)
            sp.dma_start(wo[:, :, :], a["wo"].rearrange("(c p) n -> p c n", p=128)).then_inc(s_in[3], 16)
            sp.wait_ge(s_zero, 2)
            for i in range(RI):
                for half_k in range(2):
                    r = 64 * half_k + H * i
                    sp.dma_start(w1d[r:r + H, HC * i:HC * (i + 1)], a["w1"][H * half_k:H * (half_k + 1), :]).then_inc(s_w12, 16)
                sp.dma_start(w2d[HC * i:HC * (i + 1), H * i:H * (i + 1)], a["w2"]).then_inc(s_w12, 16)

            def move_scores(b):
                for k in range(NB):
                    src, it = (S0, 0) if k < NB // 2 else (S1, 1)
                    if k == 0:
                        sp.wait_ge(s_zero, 5 + NB)
                        wait(sp, s_s0, NPAIR * (b + 1))
                    if k == NB // 2:
                        wait(sp, s_s1, NPAIR * (b + 1))
                    for par in range(2):
                        for m in range(PPB):
                            row = 32 * (k % (NB // 2)) + RP * m + RI * par
                            at = (par * PPB + m) * SLOT[k] + LEAD - RP * m
                            sp.dma_start(X[k][0:64, at:at + W[k]], src[row:row + RI, :, 0:W[k]]).then_inc(s_x[k], 16)

            move_scores(0)
            with sp.Fori(1, B) as b:
                move_scores(b)
            sp.wait_ge(s_pv, NPAIR * B)
            for dst, src in ((eg, a["egT"]), (eu, a["euT"]), (sg, a["sgT"]), (su, a["suT"]), (gwT, a["gwT"]),
                             (dn[:, 0:4, :], a["edT"].rearrange("(m p) n -> p m n", p=128)), (dn[:, 4, :], a["sdT"]),
                             (lbb, a["lbb"]), (rank, a["k_rank"])):
                sp.dma_start(dst, src).then_inc(s_inm, 16)
            sp.dma_start(S1f[0:E, 3072:3072 + 512], a["k_pick"]).then_inc(s_inm, 16)
            with sp.Fori(0, NT // 4 // 2) as r2:
                g = r2 * 2
                for u in range(2):
                    sp.wait_ge(s_r2, g + (u + 1))
                    sp.wait_ge(s_inm, 160)
                    sp.dma_start(out[ds((g + u) * 512, 512), :].rearrange("(t p) n -> p t n", p=128),
                                 res[:, u, :].rearrange("p (t n) -> p t n", n=HID)).then_inc(s_out, 16)
            sp.wait_ge(s_out, 16 * (NT // 4))

        @block.gpsimd
        def _(pool):
            pool.memset(w1d[:, :], 0.0).then_inc(s_zero, 1)
            pool.memset(w2d[:, :], 0.0).then_inc(s_zero, 1)
            pool.memset(kz[:, :, :, :], 0.0).then_inc(s_zero, 1)
            pool.memset(half[:, :], -0.5).then_inc(s_zero, 1)
            pool.memset(ones[:, :], 1.0).then_inc(s_zero, 1)
            for k in range(NB):
                pool.memset(X[k][0:64, :], 0.0).then_inc(s_zero, 1)
            pool.memset(P0[:, :, :], 0.0).then_inc(s_zero, 1)
            pool.wait_ge(s_dve0, 10)
            pool.memset(P1[:, :, :], 0.0).then_inc(s_zero, 1)

            def rstd_all(n):
                pool.wait_ge(s_st, n)
                pool.tensor_tensor(rstd[:, :], rstd[:, :], half[:, :], ALU.pow).then_inc(s_pw, 1)

            def rope_adds(b):
                for n in range(NPROJ):
                    c, u = n // 2, n // 2 % 2
                    wait(pool, s_rm, NPROJ * b + n + 1)
                    t = tmp[:, n % 2, :]
                    if n % 2 == 0:
                        wait(pool, s_sc, NSC * b + 2 * max(c - 1, 0))
                        wait(pool, s_ra, 3 * NPAIR * b + 3 * c)
                        pool.tensor_tensor(qT[:, u, :], t[:, 0:L], t[:, L:2 * L], ALU.add).then_inc(s_ra, 1)
                    else:
                        for e in range(2):
                            r = slice(64 * e, 64 * e + 64)
                            wait(pool, s_ra, 3 * NPAIR * b + 3 * c + 1 + e)
                            pool.tensor_tensor(kz[r, u, e, :], t[r, 0:L], t[r, L:2 * L], ALU.add).then_inc(s_ra, 1)

            rstd_all(1)
            rope_adds(0)
            with pool.Fori(1, B) as b:
                rope_adds(b)
            rstd_all(2)

        @block.scalar
        def _(act):
            act.wait_ge(s_in[0], 80)
            act.activation(cT[:, 1, :], cT[:, 0, :], ACT.Exp, scale=-1.0).then_inc(s_act0, 1)
            act.wait_ge(s_dve0, 1)
            act.activation(pac[:, 4:6], pac[:, 2:4], ACT.Exp, scale=-1.0).then_inc(s_act0, 1)
            act.wait_ge(s_act0, 2)
            act.activation(pac[:, 6:8], pac[:, 4:6], ACT.Ln, bias=1.0).then_inc(s_act0, 1)
            act.wait_ge(s_dve0, 5)
            kt = P1[64:128, 0:3, :].rearrange("p a b -> p (a b)")[:, 0:2 * (L + SLACK)]
            act.activation(kt, kt, ACT.Ln, scale=pac[64:128, 9:10], bias=1.0).then_inc(s_act0, 1)

            def gates_copy(done):
                with act.Fori(0, B // 2) as r2:
                    b = r2 * 2
                    for u in range(2):
                        act.wait_ge(s_gt, b + (done + u + 1))
                        act.activation(gates[:, ds(b + u, 1), :].rearrange("p a n -> p (a n)"), bank[u][:, 0:HID], ACT.Copy).then_inc(s_gd, 1)

            def modulate(which, done):
                with act.Fori(0, B // 2) as r2:
                    b = r2 * 2
                    for u in range(2):
                        act.wait_ge(s_tr, b + (done + u + 1))
                        act.activation(hT[:, ds((b + u) * L, L)], bank[2 + u][:, 0:L], ACT.Identity,
                                       scale=modc[:, 2 * which + 1, ds(b + u, 1)],
                                       bias=modc[:, 2 * which, ds(b + u, 1)]).then_inc(s_ht, 1)

            gates_copy(0)
            act.wait_ge(s_dve0, 11)
            modulate(0, 0)

            def score_copies(b, c):
                wait(act, s_sc, NSC * b + 2 * c + 2)
                if c == 0:
                    for k in range(NB // 2, NB):
                        wait(act, s_x[k], 16 * 2 * PPB * b)
                act.activation(S1[:, 2 * c:2 * c + 2, :].rearrange("p a b -> p (a b)"), bank[3][:, :], ACT.Copy, scale=SCALE).then_inc(s_s1, 1)

            def exps(b, c):
                if c == 0:
                    wait(act, s_nm, b + 1)
                    wait(act, s_n, NPAIR * b)
                for p in range(4 * c, 4 * c + 4):
                    w = row_pair_keys(p)
                    act.activation(p_slot(p)[:, 0:w], p_slot(p)[:, 0:w], ACT.Exp, bias=mx[:, p:p + 1],
                                   accum_out=rs[:, p:p + 1]).then_inc(s_e, 1)

            def finish_attention(b):
                for g in range(1, NGRP, 2):
                    wait(act, s_t, NGRP * b + g + 1)
                    if g == 1:
                        wait(act, s_pv, NPAIR * b)
                    copy_group(act, g, s_ta)
                for c in range(NPAIR):
                    wait(act, s_pv, NPAIR * b + c + 1)
                    wait(act, s_yp, NPAIR * b + max(c - 3, 0))
                    act.activation(OT[:, c % 4, :], bank[2 + c % 2][:, 0:L], ACT.Copy).then_inc(s_o, 1)

            def copy_group(eng, g, s):
                if g < NP // 4:
                    dst, q, hi = PT0, g, 0
                else:
                    dst, q, hi = PT1, g - NP // 4, 1
                o = dst[:, :, 32 * q:32 * q + 32].rearrange("p h i -> p i h")
                i_ = bank[g % 2][:, :].rearrange("p (i h) -> p i h", h=H)
                if eng is act:
                    eng.activation(o, i_, ACT.Copy).then_inc(s, 1)
                else:
                    eng.tensor_copy(o, i_).then_inc(s, 1)

            def mlp_side(b):
                for n in range(4):
                    wait(act, s_vp, 4 * b + n + 1)
                    if n == 0:
                        wait(act, s_pv, NPAIR * b)
                    act.activation(V[:, n // 2, 512 * (n % 2):512 * (n % 2) + 512], bank[n % 2][:, :], ACT.Copy).then_inc(s_v, 1)
                for c, (k, m, n, w) in enumerate(CHUNKS):
                    N = 2 * n * w
                    wait(act, s_h, NCH * b + c + 1)
                    wait(act, s_l, NCH * b + c - 1)
                    act.activation(Hs[:, c % 2, 0:N], bank[4 + c % 2][:, 0:N], ACT.Gelu, bias=b1c[:, :]).then_inc(s_g, 1)

            for c in range(NPAIR):
                score_copies(0, c)
            act.wait_ge(s_in[3], 64)
            mlp_side(0)
            with act.Fori(1, B) as b:
                for c in range(NPAIR):
                    exps(b - 1, c)
                    score_copies(b, c)
                finish_attention(b - 1)
                mlp_side(b)
            for c in range(NPAIR):
                exps(B - 1, c)
            finish_attention(B - 1)

            gates_copy(B)
            modulate(1, B)
            act.wait_ge(s_dr, 1)
            act.activation(rt[:, 1, :], rt[:, 0, :], ACT.Exp, scale=-1.0).then_inc(s_al, 1)
            with act.Fori(0, NT // 4, 1) as g:
                for m in range(5):
                    act.wait_ge(s_gp, g * 5 + (m + 1))
                    if m >= 2:
                        act.wait_ge(s_a1, g * 5 + (m - 1))
                    else:
                        act.wait_ge(s_a1, g * 5 + (m - 1 if m >= 1 else 0))
                    act.activation(sil[:, m % 2, :], bank[m % 2][:, :], ACT.Silu).then_inc(s_si, 1)

        @block.vector
        def _(dve):
            count = [0]

            def step(ins):
                count[0] += 1
                ins.then_inc(s_dve0, 1)
                dve.wait_ge(s_dve0, count[0])

            dve.wait_ge(s_in[0], 80)
            step(dve.scalar_tensor_tensor(pac[:, 2:4], pac[:, 0:2], -1.0, pac[:, 0:2], ALU.mult, ALU.max))
            dve.wait_ge(s_act0, 1)
            step(dve.tensor_scalar(cT[:, 2, :], cT[:, 1, :], 1.0, None, ALU.add))
            step(dve.reciprocal(cT[:, 1, :], cT[:, 2, :]))
            step(dve.tensor_tensor(cT[:, 3, :], cT[:, 0, :], cT[:, 1, :], ALU.mult))
            dve.wait_ge(s_act0, 3)
            step(dve.scalar_tensor_tensor(pac[:, 8:10], pac[:, 0:2], 0.0, pac[:, 6:8], ALU.max, ALU.add))
            step(dve.tensor_scalar(pac[:, 10:11], pac[:, 8:9], -1.0, None, ALU.mult))
            step(dve.tensor_copy(selx[0:64, :], ident[0:64, 0:64]))
            step(dve.tensor_copy(selx[64:128, :], ident[64:128, 64:128]))
            dve.wait_ge(s_act0, 4)
            kt = P1[64:128, 0:3, :].rearrange("p a b -> p (a b)")[:, 0:2 * (L + SLACK)]
            step(dve.tensor_scalar(kt, kt, pac[64:128, 10:11], None, ALU.mult))
            ktv = kt.rearrange("p (a t) -> p a t", a=2)
            for k in range(NB):
                for par in range(2):
                    o = X[k][64:128, par * PPB * SLOT[k]:(par + 1) * PPB * SLOT[k]].rearrange("q (m t) -> q m t", m=PPB)
                    for m in range(PPB):
                        last = dve.tensor_copy(o[:, m, :], ktv[:, par, L - W[k]:L + SLACK])
            step(last)
            dve.wait_ge(s_pe0, 1)
            for j in range(4):
                last = dve.tensor_scalar(modc[:, j, :], bank[2][:, B * j:B * (j + 1)], float(j % 2), None, ALU.add)
            step(last)
            dve.wait_ge(s_in[3], 64)
            step(dve.tensor_scalar(futb2[:, :], futb2[:, :], b2c[:, :], None, ALU.add))
            dve.wait_ge(s_zero, 5 + NB)

            def gates_spread(done):
                with dve.Fori(0, B // 2) as r2:
                    b = r2 * 2
                    for u in range(2):
                        dve.wait_ge(s_gt, b + (done + u - 1 if done + u >= 1 else 0))
                        dve.tensor_copy(cbc[:, u, :], cT[:, 3, ds(b + u, 1)].to_broadcast([128, 128])).then_inc(s_cb, 1)

            def gates_clamp(sgn):
                g = gates[:, :, :].rearrange("p a n -> p (a n)")
                step(dve.tensor_scalar(sgn, g, 0.0, 2.0, ALU.is_ge, ALU.mult))
                step(dve.scalar_tensor_tensor(g, g, -1.0, g, ALU.mult, ALU.max))
                step(dve.tensor_scalar(g, g, 0.25, None, ALU.max))
                step(dve.scalar_tensor_tensor(g, sgn, -1.0, g, ALU.add, ALU.mult))

            def norm_stats(done):
                with dve.Fori(0, NT) as t:
                    dve.bn_stats(stat[:, ds(t, 1), :].rearrange("p a n -> p (a n)"), xall[:, ds(t, 1), :].rearrange("p a n -> p (a n)")).then_inc(s_bn, 1)
                dve.wait_ge(s_bn, (done + 1) * NT + 6 * done)
                me, ve, mo, vo = (stat[:, :, j] for j in (1, 2, 4, 5))
                k = [(done + 1) * NT + 6 * done]

                def part(ins):
                    k[0] += 1
                    ins.then_inc(s_bn, 1)
                    dve.wait_ge(s_bn, k[0])
                part(dve.tensor_tensor(mean[:, :], me, mo, ALU.add))
                part(dve.tensor_scalar(mean[:, :], mean[:, :], 0.5, None, ALU.mult))
                part(dve.tensor_tensor(me, me, mo, ALU.subtract))
                part(dve.scalar_tensor_tensor(me, me, 0.25, me, ALU.mult, ALU.mult))
                part(dve.tensor_tensor(ve, ve, vo, ALU.add))
                part(dve.scalar_tensor_tensor(ve, ve, 1.0 / HID, me, ALU.mult, ALU.add))
                dve.tensor_scalar(rstd[:, :], ve, EPS_LN, None, ALU.add).then_inc(s_st, 1)

            def norm_rows(done):
                dve.wait_ge(s_pw, done // B + 1)
                with dve.Fori(0, B // 2) as r2:
                    b = r2 * 2
                    for u in range(2):
                        dve.wait_ge(s_tr, b + (done + u - 1 if done + u >= 1 else 0))
                        for t in range(TT):
                            n = (b + u) * TT + t
                            ins = dve.tensor_scalar(xn[:, u, t, :], xall[:, ds(n, 1), :].rearrange("p a n -> p (a n)"),
                                                    mean[:, ds(n, 1)], rstd[:, ds(n, 1)], ALU.subtract, ALU.mult)
                        ins.then_inc(s_xn, 1)

            gates_spread(0)
            dve.wait_ge(s_in[1], 16)
            norm_stats(0)
            norm_rows(0)
            dve.wait_ge(s_gd, B)
            gates_clamp(PT0f[:, 0:B * HID])

            def copy_group(g, s):
                dst, q = (PT0, g) if g < NP // 4 else (PT1, g - NP // 4)
                o = dst[:, :, 32 * q:32 * q + 32].rearrange("p h i -> p i h")
                dve.tensor_copy(o, bank[g % 2][:, :].rearrange("p (i h) -> p i h", h=H)).then_inc(s, 1)

            def proj_and_scores(b, soft):
                wait(dve, s_ht, b + 1 if isinstance(b, int) else B)
                wait(dve, s_vp, 4 * b)
                dve.tensor_copy(hcur[:, :], hT[:, ds(b * L, L)]).then_inc(s_hc, 1)
                for c in range(NPAIR):
                    for n in (2 * c, 2 * c + 1):
                        wait(dve, s_qk, NPROJ * b + n + 1)
                        wait(dve, s_ra, 3 * NPAIR * b + 3 * (c - 1) + (1 if n % 2 == 0 else 3))
                        dve.tensor_tensor(tmp[:, n % 2, :], bank[n % 2][:, :], rope[:, :], ALU.mult).then_inc(s_rm, 1)
                    if soft:
                        normalise(b - 1, c)
                    wait(dve, s_sc, NSC * b + 2 * c + 1)
                    if c == 0:
                        for k in range(NB // 2):
                            wait(dve, s_x[k], 16 * 2 * PPB * b)
                    dve.tensor_scalar(S0[:, 2 * c:2 * c + 2, :].rearrange("p a b -> p (a b)"), bank[2][:, 0:256], SCALE, None, ALU.mult).then_inc(s_s0, 1)

            def normalise(b, c):
                wait(dve, s_e, NP * b + 4 * c + 4)
                dve.reciprocal(rr[:, 4 * c:4 * c + 4], rs[:, 4 * c:4 * c + 4]).then_inc(s_rc, 1)
                wait(dve, s_rc, NPAIR * b + c + 1)
                for p in range(4 * c, 4 * c + 4):
                    w = row_pair_keys(p)
                    ins = dve.tensor_scalar(p_slot(p)[:, 0:w], p_slot(p)[:, 0:w], rr[:, p:p + 1], None, ALU.mult)
                ins.then_inc(s_n, 1)

            def finish_attention(b):
                for g in range(0, NGRP, 2):
                    wait(dve, s_t, NGRP * b + g + 1)
                    if g == 0:
                        wait(dve, s_pv, NPAIR * b)
                    copy_group(g, s_td)
                wait(dve, s_yp, NPAIR * (b + 1))
                for t in range(TT):
                    ins = dve.tensor_tensor(yt[:, t, :], bank[t][:, 0:HID], gates[:, ds(b, 1), :].rearrange("p a n -> p (a n)"), ALU.mult)
                ins.then_inc(s_y, 1)
                wait(dve, s_y, b + 1)
                xb = xall[:, ds(b * TT, TT), :]
                dve.tensor_tensor(xb, xb, yt[:, :, :], ALU.add).then_inc(s_x1, 1)

            def maxima(b):
                for c, (k, m, n, w) in enumerate(CHUNKS):
                    if c == 0:
                        dve.wait_ge(s_zero, 7 + NB)
                        wait(dve, s_t, NGRP * b)
                    wait(dve, s_l, NCH * b + c + 1)
                    dve.sem_inc(s_seen, 1)
                    for j in range(n):
                        p = PPB * k + m + j
                        e = row_pair_keys(p)
                        ins = dve.tensor_tensor_reduce(out=p_slot(p)[:, 0:e], in0=bank[6 + c % 2][:, j * w + w - e:j * w + w],
                                                       in1=futb2[:, L - e:L], scale=1.0, scalar=3.0 * FAR, op0=ALU.add, op1=ALU.max,
                                                       accum_out=mx[:, p:p + 1])
                    ins.then_inc(s_m, 1)
                wait(dve, s_m, NCH * (b + 1))
                dve.tensor_scalar(mx[:, :], mx[:, :], -1.0, None, ALU.mult).then_inc(s_nm, 1)

            dve.wait_ge(s_in[2], 32)
            proj_and_scores(0, False)
            maxima(0)
            with dve.Fori(1, B) as b:
                proj_and_scores(b, True)
                finish_attention(b - 1)
                maxima(b)
            for c in range(NPAIR):
                normalise(B - 1, c)
            finish_attention(B - 1)

            gates_spread(B)
            dve.wait_ge(s_x1, B)
            norm_stats(1)
            norm_rows(B)
            with dve.Fori(0, NT // 4 // 2) as r2:
                g = r2 * 2
                for u in range(2):
                    dve.wait_ge(s_lp, g + (u + 1))
                    dve.wait_ge(s_lt, g + (u - 1 if u >= 1 else 0))
                    dve.tensor_copy(lgT[:, u, :], bank[4 + u][0:E, :]).then_inc(s_lc, 1)
            dve.wait_ge(s_lt, NT // 4)
            dve.wait_ge(s_inm, 160)
            n_ = [0]

            def rstep(ins):
                n_[0] += 1
                ins.then_inc(s_dr, 1)
                dve.wait_ge(s_dr, n_[0])

            def by_e(x):
                return x.rearrange("p (t e) -> p t e", e=E)
            lg, ex, sc_, eq, fi, s2_, mk, wt = (rt[:, j, :] for j in range(8))
            rstep(dve.tensor_tensor(lg, bank[6][:, 0:NT * E], lbb, ALU.add))
            dve.wait_ge(s_al, 1)
            rstep(dve.tensor_scalar(ex, ex, 1.0, None, ALU.add))
            rstep(dve.reciprocal(sc_, ex))

            def top(of, dst, m):
                rstep(dve.tensor_reduce(m, by_e(of), AX.X, ALU.max))
                rstep(dve.tensor_tensor(by_e(eq), by_e(of), m.unsqueeze(2).to_broadcast([128, NT, E]), ALU.is_equal))
                rstep(dve.tensor_tensor(eq, eq, rank, ALU.mult))
                rstep(dve.tensor_reduce(rstd[:, :], by_e(eq), AX.X, ALU.max))
                rstep(dve.tensor_tensor(by_e(dst), by_e(eq), rstd[:, :].unsqueeze(2).to_broadcast([128, NT, E]), ALU.is_equal))
            m1, m2 = top1[:, :], top2[:, :]
            top(sc_, fi, m1)
            rstep(dve.scalar_tensor_tensor(s2_, fi, -4.0, sc_, ALU.mult, ALU.add))
            top(s2_, mk, m2)
            rstep(dve.tensor_tensor(mk, mk, fi, ALU.add))
            rstep(dve.tensor_copy(maskb[:, :], mk))
            rstep(dve.tensor_tensor(m1, m1, m2, ALU.add))
            rstep(dve.tensor_scalar(m1, m1, EPS_TOP, None, ALU.add))
            rstep(dve.reciprocal(m2, m1))
            rstep(dve.tensor_tensor(wt, mk, sc_, ALU.mult))
            rstep(dve.tensor_tensor(by_e(wt), by_e(wt), m2.unsqueeze(2).to_broadcast([128, NT, E]), ALU.mult))
            rstep(dve.tensor_reduce(tot[:, 0:E], wt.rearrange("p (t e) -> p e t", e=E), AX.X, ALU.add))
            rstep(dve.tensor_reduce(tot[:, E:2 * E], mk.rearrange("p (t e) -> p e t", e=E), AX.X, ALU.add))
            rstep(dve.tensor_copy(identb, ident[:, :]))
            rstep(dve.tensor_copy(pickb[:, :], S1f[0:E, 3072:3072 + 512]))
            assert n_[0] == ROUTER_STEPS
            dve.wait_ge(s_tp, 1)
            rstep(dve.tensor_scalar(tot[:, 2 * E:3 * E], bank[7][:, E:2 * E], 1.0, None, ALU.max))
            rstep(dve.reciprocal(tot[:, 3 * E:4 * E], tot[:, 2 * E:3 * E]))
            rstep(dve.tensor_tensor(tot[:, 0:E], tot[:, 3 * E:4 * E], bank[7][:, 0:E], ALU.mult))
            tv = tot[:, 0:E].rearrange("p (m a) -> p m a", a=2)
            rstep(dve.tensor_copy(wm[0:64, :], tv[0:64, :, 0]))
            rstep(dve.tensor_copy(wm[64:128, :], tv[64:128, :, 1]))
            for m in range(4):
                last = dve.tensor_scalar(dn[:, m, :], dn[:, m, :], wm[:, m:m + 1], None, ALU.mult)
            last.then_inc(s_wm, 1)
            dve.wait_ge(s_gd, 2 * B)
            gates_clamp(P0[:, :, :].rearrange("p a b -> p (a b)"))
            with dve.Fori(0, NT // 4 // 2) as r2:
                g = r2 * 2
                for u in range(2):
                    gg = g + u
                    dve.wait_ge(s_mtp, gg)
                    dve.tensor_copy(mcur[:, :], maskb[:, ds(gg * 4 * E, 4 * E)]).then_inc(s_mc, 1)
                    dve.wait_ge(s_mtp, gg + 1)
                    dve.wait_ge(s_mb, gg * 4)
                    dve.tensor_copy(mT[:, :], bank[5][:, :].bitcast(bf16)[0:E, 0:512]).then_inc(s_mt, 1)
                    dve.wait_ge(s_dp, gg)
                    for m in range(5):
                        dve.wait_ge(s_si, gg * 5 + (m + 1))
                        dve.wait_ge(s_up, gg * 5 + (m + 1))
                        dve.tensor_tensor(acts[:, m, :], sil[:, m % 2, :], bank[2 + m % 2][:, :], ALU.mult).then_inc(s_a1, 1)
                        if m < 4:
                            dve.wait_ge(s_a1, gg * 5 + (m + 1))
                            dve.wait_ge(s_mb, gg * 4 + (m + 1))
                            dve.tensor_tensor(acts[:, m, :], acts[:, m, :], bank[4][:, :], ALU.mult).then_inc(s_a2, 1)
                    dve.wait_ge(s_dp, gg + 1)
                    dve.wait_ge(s_out, 16 * g)
                    for t in range(4):
                        last = dve.tensor_tensor(res[:, u, HID * t:HID * (t + 1)], bank[6][:, HID * t:HID * (t + 1)],
                                                 gates[:, ds(2 * gg + t // 2, 1), :].rearrange("p a n -> p (a n)"), ALU.mult)
                    last.then_inc(s_r1, 1)
                    dve.wait_ge(s_r1, gg + 1)
                    r = res[:, u, :].rearrange("p (t n) -> p t n", n=HID)
                    dve.tensor_tensor(r, r, xall[:, ds(gg * 4, 4), :], ALU.add).then_inc(s_r2, 1)

        @block.tensor
        def _(pe):
            def mm(o, l, r, start=True, stop=True, **kw):
                return pe.matmul(o, l, r, start=start, stop=stop, **kw)

            pe.wait_ge(s_in[0], 80)
            pe.wait_ge(s_dve0, 4)
            for j, part in enumerate((0, 1, 3, 4)):
                last = mm(bank[2][:, B * j:B * (j + 1)], wmod[:, HID * part:HID * (part + 1)], cT[:, 3, :])
            last.then_inc(s_pe0, 1)

            def gates_product(part, done):
                with pe.Fori(0, B // 2) as r2:
                    b = r2 * 2
                    for u in range(2):
                        pe.wait_ge(s_cb, b + (done + u + 1))
                        pe.wait_ge(s_gd, b + (done + u - 1 if done + u >= 1 else 0))
                        mm(bank[u][:, 0:HID], cbc[:, u, :], wmod[:, HID * part:HID * (part + 1)]).then_inc(s_gt, 1)

            def norm_transposes(done):
                with pe.Fori(0, B // 2) as r2:
                    b = r2 * 2
                    for u in range(2):
                        pe.wait_ge(s_xn, b + (done + u + 1))
                        pe.wait_ge(s_ht, b + (done + u - 1 if done + u >= 1 else 0))
                        for t in range(TT):
                            last = pe.transpose(bank[2 + u][:, 128 * t:128 * (t + 1)], xn[:, u, t, :], ident[:, :])
                        last.then_inc(s_tr, 1)

            gates_product(2, 0)
            pe.wait_ge(s_dve0, 11)
            norm_transposes(0)
            pe.wait_ge(s_in[2], 32)

            def proj(b, n):
                c, base = n // 2, (0, H * D)[n % 2]
                o = bank[n % 2]
                if n < 2:
                    wait(pe, s_v, 4 * b)
                    if n == 0:
                        wait(pe, s_hc, b + 1)
                else:
                    wait(pe, s_rm, NPROJ * b + n - 1)
                w = wqkv[:, base + 128 * c:base + 128 * (c + 1)]
                mm(o[:, 0:L], w, hcur[:, :])
                for e in range(2):
                    for s in range(2):
                        col = base + 128 * c + 64 * e + 32 * (1 - s)
                        q = 64 * e + 32 * s
                        last = mm(o[q:q + 32, L:2 * L], wqkv[:, col:col + 32], hcur[:, :])
                last.then_inc(s_qk, 1)

            def scores(b, c):
                u = c % 2
                wait(pe, s_ra, 3 * NPAIR * b + 3 * (c + 1))
                if c == 0:
                    wait(pe, s_o, NPAIR * (b - 1))
                wait(pe, s_s0, NPAIR * b + c)
                mm(bank[2][:, 0:256].rearrange("p (a j) -> p a j", a=2), qT[:, u, 0:128], kz[:, u, :, 0:128]).then_inc(s_sc, 1)
                wait(pe, s_s1, NPAIR * b + c)
                mm(bank[3][:, :].rearrange("p (a j) -> p a j", a=2), qT[:, u, 128:256], kz[:, u, :, :]).then_inc(s_sc, 1)

            def proj_and_scores(b):
                proj(b, 0)
                proj(b, 1)
                for c in range(NPAIR):
                    if c + 1 < NPAIR:
                        proj(b, 2 * c + 2)
                        proj(b, 2 * c + 3)
                    scores(b, c)

            def finish_attention(b):
                for g in range(NGRP):
                    if g < 2:
                        wait(pe, s_rm, NPROJ * (b + 2) if not isinstance(b, int) or b < B - 1 else NPROJ * B)
                    elif g % 2 == 0:
                        wait(pe, s_td, (NGRP // 2) * b + g // 2)
                    else:
                        wait(pe, s_ta, (NGRP // 2) * b + g // 2)
                    q = g if g < NP // 4 else g - NP // 4 + NP // 8
                    if g < NP // 4:
                        wait(pe, s_n, NPAIR * b + g + 1)
                    hi = 0 if g < NP // 4 else 128
                    for j in range(4):
                        last = pe.transpose(bank[g % 2][:, 128 * j:128 * (j + 1)], p_slot(4 * q + j)[:, hi:hi + 128], ident[:, :])
                    last.then_inc(s_t, 1)
                wait(pe, s_td, (NGRP // 2) * (b + 1))
                wait(pe, s_ta, (NGRP // 2) * (b + 1))
                wait(pe, s_v, 4 * (b + 1))
                for c in range(NPAIR):
                    if c < 2:
                        n = NPAIR * (b + 2) if not isinstance(b, int) or b < B - 1 else NPAIR * B
                        wait(pe, s_s0, n)
                        wait(pe, s_s1, n)
                    else:
                        wait(pe, s_o, NPAIR * b + c - 1)
                    o = bank[2 + c % 2]
                    for e in range(2):
                        h, r = 2 * c + e, slice(64 * e, 64 * e + 64)
                        mm(o[r, 0:L], V[:, 0, D * h:D * (h + 1)], PT0[:, h, :], stop=False)
                        last = mm(o[r, 128:L], V[:, 1, D * h:D * (h + 1)], PT1[:, h, :], start=False)
                    last.then_inc(s_pv, 1)
                    if c >= 1:
                        output(b, c - 1)
                output(b, NPAIR - 1)

            def output(b, c):
                wait(pe, s_o, NPAIR * b + c + 1)
                for t in range(TT):
                    last = mm(bank[t][:, 0:HID], OT[:, c % 4, 128 * t:128 * (t + 1)], wo[:, c, :],
                              start=(c == 0), stop=(c == NPAIR - 1))
                last.then_inc(s_yp, 1)

            def values_and_mlp(b):
                for n in range(4):
                    if n < 2:
                        wait(pe, s_rm, NPROJ * (b + 1))
                        wait(pe, s_y, b)
                    else:
                        wait(pe, s_v, 4 * b + n - 1)
                    t, q = n // 2, n % 2
                    mm(bank[n % 2][:, :], hcur[:, 128 * t:128 * (t + 1)], wqkv[:, 2 * H * D + 512 * q:2 * H * D + 512 * (q + 1)]).then_inc(s_vp, 1)

                def hidden(c):
                    k, m, n, w = CHUNKS[c]
                    if c == CPB[k][0]:
                        wait(pe, s_x[k], 16 * 2 * PPB * (b + 1))
                    wait(pe, s_g, NCH * b + c - 1)
                    v = X[k][:, :].rearrange("q (a m t) -> q a m t", a=2, m=PPB)[:, :, m:m + n, W[k] - w:W[k]]
                    if n == 1:
                        v = v.rearrange("q a m t -> q a (m t)")
                        o = bank[4 + c % 2][:, 0:2 * w].rearrange("p (a t) -> p a t", a=2)
                    else:
                        o = bank[4 + c % 2][:, 0:2 * n * w].rearrange("p (a m t) -> p a m t", a=2, m=n)
                    mm(o, w1d[:, :], v).then_inc(s_h, 1)

                def logits(c):
                    k, m, n, w = CHUNKS[c]
                    wait(pe, s_m, NCH * b + c - 1)
                    for par in range(2):
                        mm(bank[6 + c % 2][64 * par:64 * par + 64, 0:n * w].rearrange("p (m t) -> p m t", m=n), selx[:, :],
                           x_rows(k, par, m, n, w), stop=False)
                    wait(pe, s_g, NCH * b + c + 1)
                    for par in range(2):
                        last = mm(bank[6 + c % 2][64 * par:64 * par + 64, 0:n * w], w2d[:, :],
                                  Hs[:, c % 2, par * n * w:(par + 1) * n * w], start=False)
                    last.then_inc(s_l, 1)

                hidden(0)
                for c in range(NCH):
                    if c + 1 < NCH:
                        hidden(c + 1)
                    logits(c)

            pe.wait_ge(s_gd, B)
            pe.wait_ge(s_ht, B)
            proj_and_scores(0)
            pe.wait_ge(s_w12, 16 * 3 * RI)
            pe.wait_ge(s_dve0, 10)
            values_and_mlp(0)
            with pe.Fori(1, B) as b:
                proj_and_scores(b)
                finish_attention(b - 1)
                values_and_mlp(b)
            finish_attention(B - 1)

            pe.wait_ge(s_y, B)
            gates_product(5, B)
            pe.wait_ge(s_o, NPAIR * B)
            norm_transposes(B)
            pe.wait_ge(s_inm, 160)
            pe.wait_ge(s_m, NCH * B)
            with pe.Fori(0, NT // 4 // 2) as r2:
                g = r2 * 2
                for u in range(2):
                    gg = g + u
                    pe.wait_ge(s_ht, 2 * gg + (B + 2))
                    pe.wait_ge(s_lc, g + (u - 1 if u >= 1 else 0))
                    mm(bank[4 + u][0:E, :], gwT, hT[:, ds(gg * 512, 512)]).then_inc(s_lp, 1)
                    pe.wait_ge(s_lc, gg + 1)
                    for t in range(4):
                        last = mm(bank[6][:, ds((gg * 4 + t) * E, E)], lgT[:, u, 128 * t:128 * (t + 1)], ident[0:E, 0:E])
                    last.then_inc(s_lt, 1)
            pe.wait_ge(s_dr, ROUTER_STEPS)
            mm(bank[7][:, 0:2 * E], ones[:, :], tot[:, 0:2 * E]).then_inc(s_tp, 1)
            pe.wait_ge(s_wm, 1)
            pe.wait_ge(s_gd, 2 * B)
            pe.wait_ge(s_ht, 2 * B)
            pe.wait_ge(s_lc, NT // 4)
            with pe.Fori(0, NT // 4) as g:
                pe.wait_ge(s_mc, g + 1)
                pe.wait_ge(s_mt, g)
                for t in range(4):
                    last = pe.transpose(bank[5][:, :].bitcast(bf16)[0:E, 128 * t:128 * (t + 1)], mcur[:, E * t:E * (t + 1)], identb[:, :])
                last.then_inc(s_mtp, 1)
                for m in range(5):
                    wg = eg[:, 128 * m:128 * (m + 1)] if m < 4 else sg
                    wu = eu[:, 128 * m:128 * (m + 1)] if m < 4 else su
                    pe.wait_ge(s_si, g * 5 + (m - 1 if m >= 1 else 0))
                    mm(bank[m % 2][:, :], wg, hT[:, ds(g * 512, 512)]).then_inc(s_gp, 1)
                    pe.wait_ge(s_a1, g * 5 + (m - 1 if m >= 1 else 0))
                    mm(bank[2 + m % 2][:, :], wu, hT[:, ds(g * 512, 512)]).then_inc(s_up, 1)
                    if m < 4:
                        if m == 0:
                            pe.wait_ge(s_mt, g + 1)
                        pe.wait_ge(s_a2, g * 4 + m)
                        mm(bank[4][:, :], pickb[:, 128 * m:128 * (m + 1)], mT[:, :]).then_inc(s_mb, 1)
                pe.wait_ge(s_a2, g * 4 + 4)
                pe.wait_ge(s_a1, g * 5 + 5)
                pe.wait_ge(s_r1, g)
                for t in range(4):
                    for m in range(5):
                        last = mm(bank[6][:, HID * t:HID * (t + 1)], acts[:, m, 128 * t:128 * (t + 1)], dn[:, m, :],
                                  start=(m == 0), stop=(m == 4))
                last.then_inc(s_dp, 1)


def kernel(**inputs):
    import concourse.bacc as bacc
    from concourse.bass_utils import run_bass_kernel_spmd

    v = {k.removeprefix("L0_"): np.asarray(x) for k, x in inputs.items()}
    arrays = {
        "x": v["attn_x"].reshape(B * L, HID), "wqkv": v["attn_w_qkv"], "wo": v["attn_w_o"],
        "w1": v["attn_w1"], "w2": v["attn_w2"],
        "b1": np.tile(v["attn_b1"], RI)[:, None], "b2": np.tile(v["attn_b2"], 2 * RI)[:, None],
        "pa": np.stack([np.tile(v["attn_log_p"].reshape(-1), 8), np.tile(v["attn_log_a"].reshape(-1), 8)], 1),
        "cT": v["c"].T, "wmod": v["wmod"],
        "egT": v["ffn_expert_gate_w"].reshape(E * I, HID).T, "euT": v["ffn_expert_up_w"].reshape(E * I, HID).T,
        "edT": v["ffn_expert_down_w"].transpose(0, 2, 1).reshape(E * I, HID),
        "sgT": v["ffn_shared_gate_w"].T, "suT": v["ffn_shared_up_w"].T, "sdT": v["ffn_shared_down_w"].T,
        "gwT": v["ffn_gate_w"].T, "lbb": np.tile(v["ffn_lb_bias"], (128, NT)),
    }
    arrays.update(shape_constants())
    arrays = {k: np.ascontiguousarray(x) for k, x in arrays.items()}
    nc = bacc.Bacc("TRN2", target_bir_lowering=False, num_devices=1)
    a = {k: nc.dram_tensor(f"in_{k}", x.shape, mybir.dt.from_np(x.dtype), kind="ExternalInput").ap() for k, x in arrays.items()}
    out = nc.dram_tensor("out_0", (B * L, HID), mybir.dt.float32, kind="ExternalOutput").ap()
    build(nc, a, out)
    r = run_bass_kernel_spmd(nc, [{f"in_{k}": x for k, x in arrays.items()}], core_ids=[0])
    return r.results[0]["out_0"].reshape(B, L, HID)
```

```python
import numpy as np
import concourse.bass as bass
from concourse import mybir
from contextlib import ExitStack

B, L, HID, H, D = 16, 256, 128, 16, 64
TT = L // 128
NT = B * TT
NPAIR = H // 2
E, I, TOPK = 8, 64, 2
HC = 2 * H
RI = 4
RP = 2 * RI
NP = L // RP
NB = 8
PPB = NP // NB
W = [32 * (k + 1) for k in range(NB)]
LEAD = RP * (PPB - 1)
SLACK = RP
SLOT = [w + SLACK for w in W]
CHUNKS = []
for k in range(NB):
    n = max(1, min(PPB, L // W[k]))
    for a in range(0, PPB, n):
        CHUNKS.append((k, a, n, W[k] if n > 1 else RP * (PPB * k + a + 1)))
NCH = len(CHUNKS)
NGRP = NP // 4 + NP // 8
SCALE = D ** -0.5
WS = 64.0
EPS_LN, EPS_TOP, FAR = 1e-5, 1e-8, -1e30
MODC, WSPLIT, P_FREE = 13, 18, 27
ROUTER_STEPS = 25


def row_pair_keys(p):
    return RP * (p + 1)


def shape_constants():
    f = np.float32
    inv = (f(1.0) / f(10000.0) ** (np.arange(0, D, 2, dtype=f) / f(D))).astype(f)
    ang = np.outer(np.arange(L, dtype=f), inv).astype(f)
    emb = np.concatenate([ang, ang], 1)
    cos, sin = np.cos(emb).T.astype(f), np.sin(emb).T.astype(f)
    sin[: D // 2] *= -1
    rope = np.concatenate([np.tile(cos, (2, 1)), np.tile(sin, (2, 1))], 1) / f(WS)
    row = (np.arange(128) // 64) * RI + (np.arange(128) % 64) // H
    at = np.arange(L + SLACK)[None, :] - (L - RP)
    pick = np.zeros((E, E // 2, 128), f)
    for m in range(E // 2):
        pick[2 * m, m, :64] = 1
        pick[2 * m + 1, m, 64:] = 1
    sel = np.zeros((RI, 2, H, RI, H), f)
    for i in range(RI):
        sel[i, :, np.arange(H), i, np.arange(H)] = 1
    return {
        "k_ident": np.eye(128, dtype=f), "k_rope": rope.astype(f), "k_sel": sel.reshape(128, 64),
        "k_future": np.where(at[:, :L] > row[:, None], f(FAR), f(0)).astype(f),
        "k_dist": np.abs(row[:, None] - at).astype(f), "k_pick": pick.reshape(E, -1),
        "k_rank": np.tile(E - np.arange(E, dtype=f), (128, NT)).astype(f),
    }


def build(nc, a, out):
    f32, bf16, f16 = mybir.dt.float32, mybir.dt.bfloat16, mybir.dt.float16
    ALU, ACT, AX = mybir.AluOpType, mybir.ActivationFunctionType, mybir.AxisListType
    ds = bass.ds
    ctx = ExitStack()

    def sb(name, shape, dt=f32):
        return ctx.enter_context(nc.sbuf_tensor(name, shape, dt))

    def sem(name):
        return ctx.enter_context(nc.semaphore(name))

    def wait(eng, s, v):
        if not (isinstance(v, int) and v <= 0):
            eng.wait_ge(s, v)

    with ctx:
        ident, identh = sb("ident", [128, 128]), sb("identh", [128, 128], f16)
        rope = sb("rope", [128, 2 * L])
        logadd = sb("logadd", [128, L])
        wqkv = sb("wqkv", [128, 2, 3 * H * D], f16)
        wrot = sb("wrot", [128, 2, 2 * H * D], f16)
        wo = sb("wo", [128, NPAIR, HID])
        w1s, w2d = sb("w1s", [128, 2, 128], f16), sb("w2d", [128, 64])
        sel = sb("sel", [128, 64], f16)
        hk = sb("hk", [128, 2, 2, L + SLACK], f16)
        b1c, b2c, pac = sb("b1c", [128, 1]), sb("b2c", [128, 1]), sb("pac", [128, 12])
        cT = sb("cT", [128, 4, B])
        modc = sb("modc", [128, 4, B])
        gates = sb("gates", [128, 2, B, HID])
        xall = sb("xall", [128, NT, HID])
        hT = sb("hT", [128, 2, (B + 1) * L], f16)
        mean = sb("mean", [128, NT])
        rstd, half = sb("rstd", [128, NT]), sb("half", [128, NT])
        xn, h32 = sb("xn", [128, TT, HID]), sb("h32", [128, L])
        hcur = sb("hcur", [128, 2, L], f16)
        x1 = sb("x1", [128, TT, HID])
        qT, kz = sb("qT", [128, 2, L]), sb("kz", [128, 2, 2, L])
        tmp = sb("tmp", [128, 4, 2 * L])
        V = sb("V", [128, TT, H * D])
        S0, S1 = sb("S0", [128, 2, H, 128], f16), sb("S1", [128, 2, H, L], f16)
        X = [sb(f"X{k}", [128, 2 * PPB * SLOT[k]], f16) for k in range(NB)]
        Hs = sb("Hs", [128, 2, 512])
        P0, P1 = sb("P0", [128, NP // 2, 128]), sb("P1", [128, NP // 2, L])
        mx, rs, rr = sb("mx", [128, NP]), sb("rs", [128, NP]), sb("rr", [128, NP])
        PT0, PT1 = sb("PT0", [128, H, L]), sb("PT1", [128, H, 128])
        OT = sb("OT", [128, 4, L])
        bnc = sb("bnc", [128, TT, 6])
        st2 = sb("st2", [128, 2, TT])
        rlog = sb("rlog", [128, NT * E])
        gw = sb("gw", [128, 2, E], f16)
        top1, top2 = sb("top1", [128, NT]), sb("top2", [128, NT])
        tot, wm = sb("tot", [128, 4 * E]), sb("wm", [128, 4])

        def flat(t):
            return t[:, :, :].rearrange("p a b -> p (a b)")
        PT1f, P0f, P1f, PT0f = flat(PT1), flat(P0), flat(P1), flat(PT0)
        wraw, gwraw = PT0f[:, 0:3 * H * D], P0f[:, 0:E]
        kdist, w1k, w1raw, selraw = P1f[:, 0:L + SLACK], P1f[:, 512:640], P1f[:, 640:768], P1f[:, 768:832]
        sgn = P1f[:, 1024:1024 + 2048]
        NG = (E + 2) * I
        S0f = S0[:, :, :, :].rearrange("p s h l -> p (s h l)").bitcast(f32)
        S1f = S1[:, :, :, :].rearrange("p s h l -> p (s h l)").bitcast(f32)
        cbc = S0f[:, 0:256].rearrange("p (u n) -> p u n", u=2)
        stat = S0f[:, 256:256 + 6 * NT].rearrange("p (t n) -> p t n", n=6)
        wmod = S1f[:, 0:6 * HID]
        xn1 = S1f[:, 1024:1536].rearrange("p (u t n) -> p u t n", u=2, t=TT)
        h1 = S1f[:, 1536:2048].rearrange("p (u n) -> p u n", u=2)
        eraw = S1f[:, 2048:2048 + 2 * NG]
        ew = wrot[:, :, 0:2 * NG]
        wf = wqkv[:, :, :].rearrange("p s n -> p (s n)").bitcast(f32)
        dn = wf[:, 0:5 * HID].rearrange("p (m n) -> p m n", n=HID)
        lbb, ones, rank, pickraw = wf[:, 768:1024], wf[:, 1024:1152], wf[:, 1152:1408], wf[0:E, 1408:1920]
        rt = PT1f.rearrange("p (k n) -> p k n", n=NT * E)
        Vb = V[:, 1, :].bitcast(bf16)
        maskb, mcur, mT = Vb[:, 0:NT * E], Vb[:, 256:256 + 4 * E], Vb[0:E, 512:1024]
        pickb, identb = Vb[0:E, 1024:1536], Vb[:, 1536:1664]
        acts = P1f[:, 0:5 * 512].rearrange("p (m n) -> p m n", n=512)
        sil = P0f[:, 0:1024].rearrange("p (m n) -> p m n", n=512)
        res = P0f[:, 1024:2048].rearrange("p (m n) -> p m n", n=512)

        bank = [ctx.enter_context(nc.psum_tensor(f"bank{n}", [128, 512], f32)) for n in range(8)]
        four = [bank[n] for n in (0, 1, 4, 5)]
        other = [bank[n] for n in (2, 3, 6, 7)]

        s_in = [sem(f"s_in{n}") for n in range(5)]
        s_zero = sem("s_zero")
        s_w12 = sem("s_w12")
        s_act0, s_dve0, s_pe0 = sem("s_act0"), sem("s_dve0"), sem("s_pe0")
        s_hi, s_rot = sem("s_hi"), sem("s_rot")
        s_cb, s_gt, s_gd = sem("s_cb"), sem("s_gt"), sem("s_gd")
        s_bn, s_st, s_pw, s_xn = sem("s_bn"), sem("s_st"), sem("s_pw"), sem("s_xn")
        s_tr, s_md, s_hh, s_ht = sem("s_tr"), sem("s_md"), sem("s_hh"), sem("s_ht")
        s_hc = sem("s_hc")
        s_qk, s_rm, s_ra = sem("s_qk"), sem("s_rm"), sem("s_ra")
        s_sc, s_sh, s_l0, s_l1 = sem("s_sc"), sem("s_sh"), sem("s_l0"), sem("s_l1")
        s_x = [sem(f"s_rows{k}") for k in range(NB)]
        s_vp, s_v = sem("s_vp"), sem("s_v")
        s_h, s_g, s_l, s_m = sem("s_h"), sem("s_g"), sem("s_l"), sem("s_m")
        s_nm, s_e, s_rc, s_n = sem("s_nm"), sem("s_e"), sem("s_rc"), sem("s_n")
        s_t, s_td, s_ta = sem("s_t"), sem("s_td"), sem("s_ta")
        s_pv, s_o, s_yp, s_y, s_x1 = sem("s_pv"), sem("s_o"), sem("s_yp"), sem("s_y"), sem("s_x1")
        s_xs, s_b2, s_st2, s_pw2, s_xn2 = sem("s_xs"), sem("s_b2"), sem("s_st2"), sem("s_pw2"), sem("s_xn2")
        s_tr2, s_md2, s_hh2, s_hl2, s_rp, s_rl = (sem(n) for n in ("s_tr2", "s_md2", "s_hh2", "s_hl2", "s_rp", "s_rl"))
        s_ones = sem("s_ones")
        s_seen = sem("s_seen")
        s_inm, s_ine = sem("s_inm"), sem("s_ine")
        s_eh, s_el = sem("s_eh"), sem("s_el")
        s_dr, s_al, s_tp, s_wm = sem("s_dr"), sem("s_al"), sem("s_tp"), sem("s_wm")
        s_mc, s_mtp, s_mt, s_mb = sem("s_mc"), sem("s_mtp"), sem("s_mt"), sem("s_mb")
        s_gp, s_up, s_si, s_a1, s_a2 = sem("s_gp"), sem("s_up"), sem("s_si"), sem("s_a1"), sem("s_a2")
        s_dp, s_r1, s_r2, s_out = sem("s_dp"), sem("s_r1"), sem("s_r2"), sem("s_out")

        def p_slot(p):
            return P0[:, p, :] if p < NP // 2 else P1[:, p - NP // 2, :]

        def pt_view(g):
            dst, q = (PT0, g) if g < NP // 4 else (PT1, g - NP // 4)
            return dst[:, :, 32 * q:32 * q + 32].rearrange("p h i -> p i h")

        def rows(t, n):
            return t.rearrange("p (a n) -> p a n", n=n)

        block = ctx.enter_context(nc.Block())
        FIRST = [min(c for c in range(NCH) if CHUNKS[c][0] == k) for k in range(NB)]
        NPROJ, NSC = 2 * NPAIR, 2 * NPAIR
        HG = NGRP // 2
        NORM_AT, MOD_AT, ROUTE_AT = 6, 10, 15

        @block.sync
        def _(sp):
            for dst, src in ((cT[:, 0, :], "cT"), (pac[:, 0:2], "pa"), (kdist, "k_dist"), (wmod, "wmod"),
                             (ident[:, :], "k_ident"), (selraw, "k_sel")):
                sp.dma_start(dst, a[src]).then_inc(s_in[0], 16)
            sp.dma_start(xall[:, :, :], a["x"].rearrange("(t p) n -> p t n", p=128)).then_inc(s_in[1], 16)
            sp.wait_ge(s_zero, 3)
            for i in range(RI):
                c = slice(HC * i, HC * (i + 1))
                for j in range(2):
                    sp.dma_start(w1raw[HC * i + H * j:HC * i + H * (j + 1), c], a["w1"][0:H, :]).then_inc(s_w12, 16)
                    sp.dma_start(w1k[64 * j + H * i:64 * j + H * (i + 1), c], a["w1"][H:HC, :]).then_inc(s_w12, 16)
                sp.dma_start(w2d[c, H * i:H * (i + 1)], a["w2"]).then_inc(s_w12, 16)
            sp.dma_start(wraw, a["wqkv"]).then_inc(s_in[2], 16)
            sp.dma_start(rope[:, :], a["k_rope"]).then_inc(s_in[2], 16)
            for dst, src in ((logadd[:, :], "k_future"), (b1c[:, :], "b1"), (b2c[:, :], "b2")):
                sp.dma_start(dst, a[src]).then_inc(s_in[3], 16)
            sp.dma_start(wo[:, :, :], a["wo"].rearrange("(c p) n -> p c n", p=128)).then_inc(s_in[3], 16)
            sp.dma_start(gwraw, a["gwT"]).then_inc(s_in[4], 16)

            def move_scores(b):
                sp.wait_ge(s_zero, 6 + NB)
                for k in range(NB):
                    src, it = (S0, 0) if k < NB // 2 else (S1, 1)
                    if k == 0:
                        wait(sp, s_l0, NPAIR * (b + 1))
                    if k == NB // 2:
                        wait(sp, s_l1, NPAIR * (b + 1))
                    for par in range(2):
                        for m in range(PPB):
                            row = 32 * (k % (NB // 2)) + RP * m + RI * par
                            at = (par * PPB + m) * SLOT[k] + LEAD - RP * m
                            sp.dma_start(X[k][:, at:at + W[k]], src[row:row + RI, :, :, 0:W[k]]).then_inc(s_x[k], 16)

            move_scores(0)
            with sp.Fori(1, B) as b:
                move_scores(b)
            sp.wait_ge(s_vp, 4 * B)
            for dst, src in ((lbb, "lbb"), (rank, "k_rank"), (pickraw, "k_pick"), (dn[:, 4, :], "sdT")):
                sp.dma_start(dst, a[src]).then_inc(s_inm, 16)
            sp.dma_start(dn[:, 0:4, :], a["edT"].rearrange("(m p) n -> p m n", p=128)).then_inc(s_inm, 16)
            for k in range(NB):
                sp.wait_ge(s_x[k], 16 * 2 * PPB * B)
            at = 0
            for src in ("egT", "sgT", "euT", "suT"):
                n = a[src].shape[1]
                sp.dma_start(eraw[:, at:at + n], a[src]).then_inc(s_ine, 16)
                at += n

            def store(g, u):
                sp.wait_ge(s_r2, g + u + 1)
                sp.dma_start(out[ds((g + u) * 512, 512), :].rearrange("(t p) n -> p t n", p=128),
                             rows(res[:, u, :], HID)).then_inc(s_out, 16)
            with sp.Fori(0, NT // 8) as r2:
                for u in range(2):
                    store(r2 * 2, u)
            sp.wait_ge(s_out, 16 * (NT // 4))

        @block.gpsimd
        def _(pool):
            pool.memset(w1raw, 0.0).then_inc(s_zero, 1)
            pool.memset(w1k, 0.0).then_inc(s_zero, 1)
            pool.memset(w2d[:, :], 0.0).then_inc(s_zero, 1)
            pool.memset(half[:, :], -0.5).then_inc(s_zero, 1)
            pool.memset(kz[:, :, :, :], 0.0).then_inc(s_zero, 1)
            pool.memset(hT[:, :, B * L:], 0.0).then_inc(s_zero, 1)
            for k in range(NB):
                pool.memset(X[k][:, :], 0.0).then_inc(s_zero, 1)
            pool.wait_ge(s_zero, 4)
            pool.wait_ge(s_st, 1)
            pool.tensor_tensor(rstd[:, :], rstd[:, :], half[:, :], ALU.pow).then_inc(s_pw, 1)
            pool.wait_ge(s_dve0, WSPLIT)
            for j in range(2):
                src = wqkv[:, j, 0:2 * H * D].rearrange("p (h s d) -> p h s d", s=2, d=32)
                dst = wrot[:, j, :].rearrange("p (h s d) -> p h s d", s=2, d=32)
                for s in range(2):
                    pool.tensor_copy(dst[:, :, s, :], src[:, :, 1 - s, :]).then_inc(s_rot, 1)
            pool.wait_ge(s_dve0, P_FREE)
            pool.memset(P0[:, :, :], 0.0).then_inc(s_zero, 1)
            pool.memset(P1[:, :, :], 0.0).then_inc(s_zero, 1)

            def rope_adds(b):
                for n in range(NPROJ):
                    c, u = n // 2, n // 2 % 2
                    wait(pool, s_rm, NPROJ * b + n + 1)
                    t = tmp[:, n % 4, :]
                    if n % 2 == 0:
                        if c >= 2 or not isinstance(b, int):
                            wait(pool, s_sc, NSC * b + 2 * max(c - 1, 0))
                        wait(pool, s_ra, 3 * NPAIR * b + 3 * c)
                        pool.tensor_tensor(qT[:, u, :], t[:, 0:L], t[:, L:2 * L], ALU.add).then_inc(s_ra, 1)
                    else:
                        for e in range(2):
                            r = slice(64 * e, 64 * e + 64)
                            wait(pool, s_ra, 3 * NPAIR * b + 3 * c + 1 + e)
                            pool.tensor_tensor(kz[r, u, e, :], t[r, 0:L], t[r, L:2 * L], ALU.add).then_inc(s_ra, 1)

            def second_norm(b):
                wait(pool, s_x1, b + 1)
                pool.tensor_copy(xall[:, ds(b * TT, TT), :], x1[:, :, :]).then_inc(s_xs, 1)
                wait(pool, s_st2, b + 1)
                pool.tensor_tensor(st2[:, 1, :], st2[:, 1, :], half[:, 0:TT], ALU.pow).then_inc(s_pw2, 1)

            rope_adds(0)
            with pool.Fori(1, B) as b:
                rope_adds(b)
                second_norm(b - 1)
            second_norm(B - 1)
            pool.wait_ge(s_vp, 4 * B)
            pool.memset(ones, 1.0).then_inc(s_ones, 1)

        @block.scalar
        def _(act):
            act.wait_ge(s_in[0], 96)
            act.activation(cT[:, 1, :], cT[:, 0, :], ACT.Exp, scale=-1.0).then_inc(s_act0, 1)
            act.wait_ge(s_dve0, 1)
            act.activation(pac[:, 4:6], pac[:, 2:4], ACT.Exp, scale=-1.0).then_inc(s_act0, 1)
            act.wait_ge(s_act0, 2)
            act.activation(pac[:, 6:8], pac[:, 4:6], ACT.Ln, bias=1.0).then_inc(s_act0, 1)
            act.wait_ge(s_dve0, 5)
            act.activation(kdist, kdist, ACT.Ln, scale=pac[:, 9:10], bias=1.0).then_inc(s_act0, 1)
            act.wait_ge(s_in[2], 32)
            act.activation(wqkv[:, 0, :], wraw, ACT.Copy, scale=WS).then_inc(s_hi, 1)
            act.wait_ge(s_in[4], 16)
            act.activation(gw[:, 0, :], gwraw, ACT.Copy, scale=WS).then_inc(s_hi, 1)

            def gates_copy(b, u):
                act.wait_ge(s_gt, b + u + 1)
                act.activation(gates[:, :, ds(b + u, 1), :].rearrange("p g a n -> p (g a) n"), rows(bank[u][:, 0:2 * HID], HID), ACT.Copy).then_inc(s_gd, 1)
            with act.Fori(0, B // 2) as r2:
                for u in range(2):
                    gates_copy(r2 * 2, u)

            act.wait_ge(s_dve0, MODC)

            def modulate(b, u):
                act.wait_ge(s_tr, b + u + 1)
                wait(act, s_ht, b + u - 1)
                act.activation(h1[:, u, :], bank[2 + u][:, 0:L], ACT.Identity,
                               scale=modc[:, 1, ds(b + u, 1)], bias=modc[:, 0, ds(b + u, 1)]).then_inc(s_md, 1)
                act.wait_ge(s_md, b + u + 1)
                act.activation(hT[:, 0, ds((b + u) * L, L)], h1[:, u, :], ACT.Copy).then_inc(s_hh, 1)
            for u in range(2):
                modulate(0, u)
            with act.Fori(1, B // 2) as r2:
                for u in range(2):
                    modulate(r2 * 2, u)

            def score_highs(b, c):
                wait(act, s_sc, NSC * b + 2 * c + 1)
                if c == 0:
                    for k in range(NB):
                        wait(act, s_x[k], 16 * 2 * PPB * b)
                act.activation(S0[:, 0, 2 * c:2 * c + 2, :], rows(bank[(2, 6)[c % 2]][:, 0:256], 128), ACT.Copy, scale=SCALE).then_inc(s_sh, 1)
                wait(act, s_sc, NSC * b + 2 * c + 2)
                act.activation(S1[:, 0, 2 * c:2 * c + 2, :], rows(bank[(3, 7)[c % 2]][:, :], L), ACT.Copy, scale=SCALE).then_inc(s_sh, 1)

            def exps(b, c):
                if c == 0:
                    wait(act, s_nm, b + 1)
                for p in range(4 * c, 4 * c + 4):
                    w = row_pair_keys(p)
                    act.activation(p_slot(p)[:, 0:w], p_slot(p)[:, 0:w], ACT.Exp, bias=mx[:, p:p + 1],
                                   accum_out=rs[:, p:p + 1]).then_inc(s_e, 1)

            def finish_attention(b):
                for g in range(1, NGRP, 2):
                    wait(act, s_t, NGRP * b + g + 1)
                    act.activation(pt_view(g), rows(four[g % 4][:, :], H), ACT.Copy).then_inc(s_ta, 1)
                for c in range(NPAIR):
                    if c >= 4:
                        wait(act, s_yp, NPAIR * b + c - 3)
                    wait(act, s_pv, NPAIR * b + c + 1)
                    act.activation(OT[:, c % 4, :], other[c % 4][:, 0:L], ACT.Copy).then_inc(s_o, 1)

            def second_modulate(b):
                wait(act, s_tr2, b + 1)
                act.activation(h32[:, :], bank[0][:, 0:L], ACT.Identity,
                               scale=modc[:, 3, ds(b, 1)], bias=modc[:, 2, ds(b, 1)]).then_inc(s_md2, 1)

            def mlp_side(b, norm):
                for n in range(4):
                    wait(act, s_vp, 4 * b + n + 1)
                    act.activation(V[:, n // 2, 512 * (n % 2):512 * (n % 2) + 512], bank[2 + n % 2][:, :], ACT.Copy, scale=1 / WS).then_inc(s_v, 1)
                for c, (k, m, n, w) in enumerate(CHUNKS):
                    N = 2 * n * w
                    if c >= 2:
                        wait(act, s_l, NCH * b + c - 1)
                    wait(act, s_h, NCH * b + c + 1)
                    act.activation(Hs[:, c % 2, 0:N], bank[4 + c % 2][:, 0:N], ACT.Gelu, bias=b1c[:, :], scale=1 / WS).then_inc(s_g, 1)
                    if norm and c == MOD_AT:
                        second_modulate(b - 1)

            for c in range(NPAIR):
                score_highs(0, c)
            act.wait_ge(s_in[3], 64)
            mlp_side(0, False)
            with act.Fori(1, B) as b:
                for c in range(NPAIR):
                    score_highs(b, c)
                    exps(b - 1, c)
                finish_attention(b - 1)
                mlp_side(b, True)
            for c in range(NPAIR):
                exps(B - 1, c)
            finish_attention(B - 1)
            second_modulate(B - 1)
            act.wait_ge(s_ine, 64)
            act.activation(ew[:, 0, :], eraw, ACT.Copy, scale=WS).then_inc(s_eh, 1)

            act.wait_ge(s_dr, 1)
            act.activation(rt[:, 1, :], rlog[:, :], ACT.Exp, scale=-1.0).then_inc(s_al, 1)

            def silus(g):
                for m in range(5):
                    if m >= 2 or not isinstance(g, int):
                        wait(act, s_a1, g * 5 + m - 1)
                    wait(act, s_gp, g * 5 + m + 1)
                    act.activation(sil[:, m % 2, :], bank[m % 2][:, :], ACT.Silu, scale=1 / WS).then_inc(s_si, 1)
            silus(0)
            with act.Fori(1, NT // 4) as g:
                silus(g)

        @block.vector
        def _(dve):
            count = [0]

            def step(ins):
                count[0] += 1
                ins.then_inc(s_dve0, 1)
                dve.wait_ge(s_dve0, count[0])

            dve.wait_ge(s_in[0], 96)
            step(dve.scalar_tensor_tensor(pac[:, 2:4], pac[:, 0:2], -1.0, pac[:, 0:2], ALU.mult, ALU.max))
            dve.wait_ge(s_act0, 1)
            step(dve.tensor_scalar(cT[:, 2, :], cT[:, 1, :], 1.0, None, ALU.add))
            step(dve.reciprocal(cT[:, 1, :], cT[:, 2, :]))
            step(dve.tensor_tensor(cT[:, 3, :], cT[:, 0, :], cT[:, 1, :], ALU.mult))
            dve.wait_ge(s_act0, 3)
            step(dve.scalar_tensor_tensor(pac[:, 8:10], pac[:, 0:2], 0.0, pac[:, 6:8], ALU.max, ALU.add))
            step(dve.tensor_scalar(pac[:, 10:11], pac[:, 8:9], -1.0, None, ALU.mult))
            step(dve.tensor_copy(identh[:, :], ident[:, :]))
            step(dve.tensor_copy(sel[:, :], selraw))
            def spread(b, u):
                wait(dve, s_gt, b + u - 1)
                dve.tensor_copy(cbc[:, u, :], cT[:, 3, ds(b + u, 1)].to_broadcast([128, 128])).then_inc(s_cb, 1)
            for u in range(2):
                spread(0, u)
            with dve.Fori(1, B // 2) as r2:
                for u in range(2):
                    spread(r2 * 2, u)
            dve.wait_ge(s_in[1], 16)
            for t in range(NT):
                dve.bn_stats(stat[:, t, :], xall[:, t, :]).then_inc(s_bn, 1)
            dve.wait_ge(s_bn, NT)

            def variances(st, mean_, var, s, at, n0):
                me, ve, mo, vo = (st[:, :, j] for j in (1, 2, 4, 5))
                k = [0]

                def part(ins):
                    k[0] += 1
                    ins.then_inc(s, 1)
                    wait(dve, s, at + n0 + k[0])
                part(dve.tensor_tensor(mean_, me, mo, ALU.add))
                part(dve.tensor_scalar(mean_, mean_, 0.5, None, ALU.mult))
                part(dve.tensor_tensor(me, me, mo, ALU.subtract))
                part(dve.scalar_tensor_tensor(me, me, 0.25, me, ALU.mult, ALU.mult))
                part(dve.tensor_tensor(ve, ve, vo, ALU.add))
                part(dve.scalar_tensor_tensor(ve, ve, 1.0 / HID, me, ALU.mult, ALU.add))
                return dve.tensor_scalar(var, ve, EPS_LN, None, ALU.add)
            variances(stat, mean[:, :], rstd[:, :], s_bn, 0, NT).then_inc(s_st, 1)
            dve.wait_ge(s_act0, 4)
            step(dve.tensor_scalar(kdist, kdist, pac[:, 10:11], None, ALU.mult))
            dve.wait_ge(s_in[3], 64)
            step(dve.scalar_tensor_tensor(logadd[:, :], logadd[:, :], b2c[:, :], kdist[:, 0:L], ALU.add, ALU.add))
            dve.wait_ge(s_w12, 16 * 5 * RI)
            step(dve.tensor_scalar(w1s[:, 0, :], w1raw, WS, None, ALU.mult))
            step(dve.scalar_tensor_tensor(w1s[:, 1, :], w1raw, WS, w1s[:, 0, :], ALU.mult, ALU.subtract))
            dve.wait_ge(s_pe0, 1)
            for j in range(4):
                last = dve.tensor_scalar(modc[:, j, :], bank[2][:, B * j:B * (j + 1)], float(j % 2), None, ALU.add)
            step(last)
            assert count[0] == MODC
            dve.wait_ge(s_pe0, 2)
            for par in range(2):
                step(dve.tensor_scalar(hk[:, 0, par, :], bank[4 + par][:, 0:L + SLACK], WS, None, ALU.mult))
                step(dve.scalar_tensor_tensor(hk[:, 1, par, :], bank[4 + par][:, 0:L + SLACK], WS, hk[:, 0, par, :], ALU.mult, ALU.subtract))
            dve.wait_ge(s_hi, 1)
            step(dve.scalar_tensor_tensor(wqkv[:, 1, :], wraw, WS, wqkv[:, 0, :], ALU.mult, ALU.subtract))
            assert count[0] == WSPLIT
            dve.wait_ge(s_hi, 2)
            step(dve.scalar_tensor_tensor(gw[:, 1, :], gwraw, WS, gw[:, 0, :], ALU.mult, ALU.subtract))
            dve.wait_ge(s_gd, B)
            for j in range(2):
                g = gates[:, j, :, :].rearrange("p a n -> p (a n)")
                step(dve.tensor_scalar(sgn, g, 0.0, 2.0, ALU.is_ge, ALU.mult))
                step(dve.scalar_tensor_tensor(g, g, -1.0, g, ALU.mult, ALU.max))
                step(dve.tensor_scalar(g, g, 0.25, None, ALU.max))
                step(dve.scalar_tensor_tensor(g, sgn, -1.0, g, ALU.add, ALU.mult))
            assert count[0] == P_FREE

            dve.wait_ge(s_pw, 1)

            def norm_rows(b, u):
                wait(dve, s_tr, b + u - 1)
                for t in range(TT):
                    n = (b + u) * TT + t
                    ins = dve.tensor_scalar(xn1[:, u, t, :], xall[:, ds(n, 1), :].rearrange("p a n -> p (a n)"),
                                            mean[:, ds(n, 1)], rstd[:, ds(n, 1)], ALU.subtract, ALU.mult)
                ins.then_inc(s_xn, 1)

            def low_part(b, u):
                wait(dve, s_hh, b + u + 1)
                dve.tensor_tensor(hT[:, 1, ds((b + u) * L, L)], h1[:, u, :], hT[:, 0, ds((b + u) * L, L)], ALU.subtract).then_inc(s_ht, 1)
            for u in range(2):
                norm_rows(0, u)
            with dve.Fori(1, B // 2) as r2:
                for u in range(2):
                    low_part(r2 * 2 - 2, u)
                    norm_rows(r2 * 2, u)
            for u in range(2):
                low_part(B - 2, u)

            def proj_and_scores(b, soft):
                def products(c):
                    for n in (2 * c, 2 * c + 1):
                        if n >= 4 or not isinstance(b, int):
                            wait(dve, s_ra, 3 * NPAIR * b + 3 * (c - 2) + (1 if n % 2 == 0 else 3))
                        wait(dve, s_qk, NPROJ * b + n + 1)
                        dve.tensor_tensor(tmp[:, n % 4, :], four[n % 4][:, :], rope[:, :], ALU.mult).then_inc(s_rm, 1)
                products(0)
                products(1)
                for c in range(NPAIR):
                    if c + 2 < NPAIR:
                        products(c + 2)
                    wait(dve, s_sh, NSC * b + 2 * c + 1)
                    dve.scalar_tensor_tensor(S0[:, 1, 2 * c:2 * c + 2, :], rows(bank[(2, 6)[c % 2]][:, 0:256], 128), SCALE,
                                             S0[:, 0, 2 * c:2 * c + 2, :], ALU.mult, ALU.subtract).then_inc(s_l0, 1)
                    wait(dve, s_sh, NSC * b + 2 * c + 2)
                    dve.scalar_tensor_tensor(S1[:, 1, 2 * c:2 * c + 2, :], rows(bank[(3, 7)[c % 2]][:, :], L), SCALE,
                                             S1[:, 0, 2 * c:2 * c + 2, :], ALU.mult, ALU.subtract).then_inc(s_l1, 1)
                    if soft:
                        normalise(b - 1, c)

            def normalise(b, c):
                wait(dve, s_e, NP * b + 4 * c + 4)
                dve.reciprocal(rr[:, 4 * c:4 * c + 4], rs[:, 4 * c:4 * c + 4]).then_inc(s_rc, 1)
                wait(dve, s_rc, NPAIR * b + c + 1)
                for p in range(4 * c, 4 * c + 4):
                    w = row_pair_keys(p)
                    ins = dve.tensor_scalar(p_slot(p)[:, 0:w], p_slot(p)[:, 0:w], rr[:, p:p + 1], None, ALU.mult)
                ins.then_inc(s_n, 1)

            def finish_attention(b):
                for g in range(0, NGRP, 2):
                    wait(dve, s_t, NGRP * b + g + 1)
                    dve.tensor_copy(pt_view(g), rows(four[g % 4][:, :], H)).then_inc(s_td, 1)
                wait(dve, s_yp, NPAIR * (b + 1))
                ga = gates[:, 0, ds(b, 1), :].rearrange("p a n -> p (a n)")
                for t in range(TT):
                    ins = dve.tensor_tensor(xn[:, t, :], bank[t][:, 0:HID], ga, ALU.mult)
                ins.then_inc(s_y, 1)
                wait(dve, s_y, b + 1)
                dve.tensor_tensor(x1[:, :, :], xall[:, ds(b * TT, TT), :], xn[:, :, :], ALU.add).then_inc(s_x1, 1)
                wait(dve, s_x1, b + 1)
                for t in range(TT):
                    dve.bn_stats(bnc[:, t, :], x1[:, t, :]).then_inc(s_b2, 1)
                wait(dve, s_b2, 8 * b + 2)
                variances(bnc, st2[:, 0, :], st2[:, 1, :], s_b2, 8 * b, 2).then_inc(s_st2, 1)

            def second_rows(b):
                wait(dve, s_pw2, b + 1)
                for t in range(TT):
                    ins = dve.tensor_scalar(xn[:, t, :], x1[:, t, :], st2[:, 0, t:t + 1], st2[:, 1, t:t + 1], ALU.subtract, ALU.mult)
                ins.then_inc(s_xn2, 1)

            def second_parts(b):
                wait(dve, s_md2, b + 1)
                dve.tensor_copy(hcur[:, 0, :], h32[:, :]).then_inc(s_hh2, 1)
                wait(dve, s_hh2, b + 1)
                dve.tensor_tensor(hcur[:, 1, :], h32[:, :], hcur[:, 0, :], ALU.subtract).then_inc(s_hl2, 1)
                wait(dve, s_hl2, b + 1)
                dve.tensor_copy(hT[:, :, ds(b * L, L)], hcur[:, :, :]).then_inc(s_ht, 1)

            def second_logits(b):
                wait(dve, s_rp, b + 1)
                dve.tensor_scalar(rlog[:, ds(b * TT * E, TT * E)], bank[1][:, 0:TT * E], 1 / WS, None, ALU.mult).then_inc(s_rl, 1)

            def maxima(b, norm):
                for c, (k, m, n, w) in enumerate(CHUNKS):
                    if c == 0:
                        dve.wait_ge(s_zero, 8 + NB)
                    wait(dve, s_l, NCH * b + c + 1)
                    dve.sem_inc(s_seen, 1)
                    for j in range(n):
                        p = PPB * k + m + j
                        e = row_pair_keys(p)
                        ins = dve.tensor_tensor_reduce(out=p_slot(p)[:, 0:e], in0=bank[6 + c % 2][:, j * w + w - e:j * w + w],
                                                       in1=logadd[:, L - e:L], scale=1.0, scalar=3.0 * FAR, op0=ALU.add, op1=ALU.max,
                                                       accum_out=mx[:, p:p + 1])
                    ins.then_inc(s_m, 1)
                    if norm and c == NORM_AT - 3:
                        second_rows(b - 1)
                    if norm and c == MOD_AT + 2:
                        second_parts(b - 1)
                    if norm and c == ROUTE_AT + 2:
                        second_logits(b - 1)
                    if c == ROUTE_AT + 3:
                        take_batch(b + 1)
                wait(dve, s_m, NCH * (b + 1))
                dve.tensor_scalar(mx[:, :], mx[:, :], -1.0, None, ALU.mult).then_inc(s_nm, 1)

            def take_batch(b):
                dve.tensor_copy(hcur[:, :, :], hT[:, :, ds(b * L, L)]).then_inc(s_hc, 1)

            take_batch(0)
            proj_and_scores(0, False)
            maxima(0, False)
            with dve.Fori(1, B) as b:
                proj_and_scores(b, True)
                finish_attention(b - 1)
                maxima(b, True)
            for c in range(NPAIR):
                normalise(B - 1, c)
            finish_attention(B - 1)
            second_rows(B - 1)
            second_parts(B - 1)
            second_logits(B - 1)

            dve.wait_ge(s_rl, B)
            dve.wait_ge(s_inm, 80)
            n_ = [0]

            def rstep(ins):
                n_[0] += 1
                ins.then_inc(s_dr, 1)
                dve.wait_ge(s_dr, n_[0])

            def by_e(x):
                return x.rearrange("p (t e) -> p t e", e=E)
            ex, sc_, eq, fi, s2_, mk, wt = (rt[:, j, :] for j in range(1, 8))
            rstep(dve.tensor_tensor(rlog[:, :], rlog[:, :], lbb, ALU.add))
            dve.wait_ge(s_al, 1)
            rstep(dve.tensor_scalar(ex, ex, 1.0, None, ALU.add))
            rstep(dve.reciprocal(sc_, ex))

            def top(of, dst, m):
                rstep(dve.tensor_reduce(m, by_e(of), AX.X, ALU.max))
                rstep(dve.tensor_tensor(by_e(eq), by_e(of), m.unsqueeze(2).to_broadcast([128, NT, E]), ALU.is_equal))
                rstep(dve.tensor_tensor(eq, eq, rank, ALU.mult))
                rstep(dve.tensor_reduce(rstd[:, :], by_e(eq), AX.X, ALU.max))
                rstep(dve.tensor_tensor(by_e(dst), by_e(eq), rstd[:, :].unsqueeze(2).to_broadcast([128, NT, E]), ALU.is_equal))
            m1, m2 = top1[:, :], top2[:, :]
            top(sc_, fi, m1)
            rstep(dve.scalar_tensor_tensor(s2_, fi, -4.0, sc_, ALU.mult, ALU.add))
            top(s2_, mk, m2)
            rstep(dve.tensor_tensor(mk, mk, fi, ALU.add))
            rstep(dve.tensor_copy(maskb, mk))
            rstep(dve.tensor_tensor(m1, m1, m2, ALU.add))
            rstep(dve.tensor_scalar(m1, m1, EPS_TOP, None, ALU.add))
            rstep(dve.reciprocal(m2, m1))
            rstep(dve.tensor_tensor(wt, mk, sc_, ALU.mult))
            rstep(dve.tensor_tensor(by_e(wt), by_e(wt), m2.unsqueeze(2).to_broadcast([128, NT, E]), ALU.mult))
            rstep(dve.tensor_reduce(tot[:, 0:E], wt.rearrange("p (t e) -> p e t", e=E), AX.X, ALU.add))
            rstep(dve.tensor_reduce(tot[:, E:2 * E], mk.rearrange("p (t e) -> p e t", e=E), AX.X, ALU.add))
            rstep(dve.tensor_copy(identb, ident[:, :]))
            rstep(dve.tensor_copy(pickb, pickraw))
            assert n_[0] == ROUTER_STEPS
            dve.wait_ge(s_eh, 1)
            dve.scalar_tensor_tensor(ew[:, 1, :], eraw, WS, ew[:, 0, :], ALU.mult, ALU.subtract).then_inc(s_el, 1)
            dve.wait_ge(s_tp, 1)
            rstep(dve.tensor_scalar(tot[:, 2 * E:3 * E], bank[7][:, E:2 * E], 1.0, None, ALU.max))
            rstep(dve.reciprocal(tot[:, 3 * E:4 * E], tot[:, 2 * E:3 * E]))
            rstep(dve.tensor_tensor(tot[:, 0:E], tot[:, 3 * E:4 * E], bank[7][:, 0:E], ALU.mult))
            tv = tot[:, 0:E].rearrange("p (m a) -> p m a", a=2)
            rstep(dve.tensor_copy(wm[0:64, :], tv[0:64, :, 0]))
            rstep(dve.tensor_copy(wm[64:128, :], tv[64:128, :, 1]))
            for m in range(4):
                last = dve.tensor_scalar(dn[:, m, :], dn[:, m, :], wm[:, m:m + 1], None, ALU.mult)
            last.then_inc(s_wm, 1)

            def experts(g, u):
                gg = g + u
                first = isinstance(gg, int) and gg == 0
                wait(dve, s_mtp, gg)
                dve.tensor_copy(mcur, maskb[:, ds(gg * 4 * E, 4 * E)]).then_inc(s_mc, 1)
                wait(dve, s_mb, gg * 4)
                wait(dve, s_mtp, gg + 1)
                dve.tensor_copy(mT, bank[5][:, :].bitcast(bf16)[0:E, 0:512]).then_inc(s_mt, 1)
                wait(dve, s_dp, gg)
                for m in range(5):
                    wait(dve, s_si, gg * 5 + m + 1)
                    wait(dve, s_up, gg * 5 + m + 1)
                    dve.scalar_tensor_tensor(acts[:, m, :], bank[2 + m % 2][:, :], 1 / WS, sil[:, m % 2, :], ALU.mult, ALU.mult).then_inc(s_a1, 1)
                    if m < 4:
                        wait(dve, s_a1, gg * 5 + m + 1)
                        wait(dve, s_mb, gg * 4 + m + 1)
                        dve.tensor_tensor(acts[:, m, :], acts[:, m, :], bank[4][:, :], ALU.mult).then_inc(s_a2, 1)
                if not isinstance(gg, int):
                    wait(dve, s_out, 16 * g)
                wait(dve, s_dp, gg + 1)
                for t in range(4):
                    last = dve.tensor_tensor(res[:, u, HID * t:HID * (t + 1)], bank[6][:, HID * t:HID * (t + 1)],
                                             gates[:, 1, ds(2 * gg + t // 2, 1), :].rearrange("p a n -> p (a n)"), ALU.mult)
                last.then_inc(s_r1, 1)
                wait(dve, s_r1, gg + 1)
                r = rows(res[:, u, :], HID)
                dve.tensor_tensor(r, r, xall[:, ds(gg * 4, 4), :], ALU.add).then_inc(s_r2, 1)
            experts(0, 0)
            experts(0, 1)
            with dve.Fori(1, NT // 8) as r2:
                for u in range(2):
                    experts(r2 * 2, u)

        @block.tensor
        def _(pe):
            def mm(o, l, r, start=True, stop=True, **kw):
                return pe.matmul(o, l, r, start=start, stop=stop, **kw)

            def mm3(o, l, r):
                mm(o, l(0), r(0), stop=False)
                mm(o, l(0), r(1), start=False, stop=False)
                return mm(o, l(1), r(0), start=False)

            pe.wait_ge(s_in[0], 96)
            pe.wait_ge(s_dve0, 4)
            for j, part in enumerate((0, 1, 3, 4)):
                last = mm(bank[2][:, B * j:B * (j + 1)], wmod[:, HID * part:HID * (part + 1)], cT[:, 3, :])
            last.then_inc(s_pe0, 1)

            def gates_product(b, u):
                wait(pe, s_gd, b + u - 1)
                pe.wait_ge(s_cb, b + u + 1)
                for j, part in enumerate((2, 5)):
                    last = mm(bank[u][:, HID * j:HID * (j + 1)], cbc[:, u, :], wmod[:, HID * part:HID * (part + 1)])
                last.then_inc(s_gt, 1)
            for u in range(2):
                gates_product(0, u)
            with pe.Fori(1, B // 2) as r2:
                for u in range(2):
                    gates_product(r2 * 2, u)
            pe.wait_ge(s_dve0, MODC)
            for par in range(2):
                r = slice(64 * par, 64 * par + 64)
                last = mm(bank[4 + par][:, 0:L + SLACK], w1k[r, :], kdist[r, :])
            last.then_inc(s_pe0, 1)

            def norm_transposes(b, u):
                wait(pe, s_md, b + u - 1)
                wait(pe, s_xn, b + u + 1)
                for t in range(TT):
                    last = pe.transpose(bank[2 + u][:, 128 * t:128 * (t + 1)], xn1[:, u, t, :], ident[:, :])
                last.then_inc(s_tr, 1)
            for u in range(2):
                norm_transposes(0, u)
            with pe.Fori(1, B // 2) as r2:
                for u in range(2):
                    norm_transposes(r2 * 2, u)

            def proj(b, n):
                c, base = n // 2, (0, H * D)[n % 2]
                o = four[n % 4]
                if n == 0:
                    wait(pe, s_hc, b + 1)
                if n >= 4:
                    wait(pe, s_rm, NPROJ * b + n - 3)
                at = base + 128 * c
                mm3(o[:, 0:L], lambda j: wqkv[:, j, at:at + 128], lambda j: hcur[:, j, :])
                mm3(o[:, L:2 * L], lambda j: wrot[:, j, at:at + 128], lambda j: hcur[:, j, :]).then_inc(s_qk, 1)

            def scores(b, c):
                u = c % 2
                wait(pe, s_ra, 3 * NPAIR * b + 3 * (c + 1))
                if c == 0:
                    wait(pe, s_v, 4 * b)
                if c == 1:
                    wait(pe, s_m, NCH * b)
                if c >= 2:
                    wait(pe, s_l0, NPAIR * b + c - 1)
                mm(rows(bank[(2, 6)[u]][:, 0:256], 128), qT[:, u, 0:128], kz[:, u, :, 0:128]).then_inc(s_sc, 1)
                if c >= 2:
                    wait(pe, s_l1, NPAIR * b + c - 1)
                mm(rows(bank[(3, 7)[u]][:, :], L), qT[:, u, 128:256], kz[:, u, :, :]).then_inc(s_sc, 1)

            def proj_and_scores(b):
                for n in range(4):
                    proj(b, n)
                for c in range(NPAIR):
                    if c + 2 < NPAIR:
                        proj(b, 2 * c + 4)
                        proj(b, 2 * c + 5)
                    scores(b, c)

            def finish_attention(b, done):
                for g in range(NGRP):
                    if g >= 4:
                        wait(pe, (s_td, s_ta)[g % 2], HG * b + g // 2 - 1)
                    q = g if g < NP // 4 else g - NP // 4 + NP // 8
                    if g < NP // 4:
                        wait(pe, s_n, NPAIR * b + g + 1)
                    hi = 0 if g < NP // 4 else 128
                    for j in range(4):
                        last = pe.transpose(four[g % 4][:, 128 * j:128 * (j + 1)], p_slot(4 * q + j)[:, hi:hi + 128], ident[:, :])
                    last.then_inc(s_t, 1)
                wait(pe, s_td, HG * (b + 1))
                wait(pe, s_ta, HG * (b + 1))
                wait(pe, s_v, 4 * (b + 1))
                wait(pe, s_l0, NPAIR * done)
                wait(pe, s_l1, NPAIR * done)
                for c in range(NPAIR):
                    if c >= 4:
                        wait(pe, s_o, NPAIR * b + c - 3)
                    o = other[c % 4]
                    for e in range(2):
                        h, r = 2 * c + e, slice(64 * e, 64 * e + 64)
                        mm(o[r, 0:L], V[:, 0, D * h:D * (h + 1)], PT0[:, h, :], stop=False)
                        last = mm(o[r, 128:L], V[:, 1, D * h:D * (h + 1)], PT1[:, h, :], start=False)
                    last.then_inc(s_pv, 1)
                    if c >= 1:
                        output(b, c - 1)
                output(b, NPAIR - 1)

            def output(b, c):
                wait(pe, s_o, NPAIR * b + c + 1)
                for t in range(TT):
                    last = mm(bank[t][:, 0:HID], OT[:, c % 4, 128 * t:128 * (t + 1)], wo[:, c, :],
                              start=(c == 0), stop=(c == NPAIR - 1))
                last.then_inc(s_yp, 1)

            def second_transposes(b):
                wait(pe, s_xn2, b + 1)
                for t in range(TT):
                    last = pe.transpose(bank[0][:, 128 * t:128 * (t + 1)], xn[:, t, :], ident[:, :])
                last.then_inc(s_tr2, 1)

            def route(b):
                wait(pe, s_hl2, b + 1)
                for t in range(TT):
                    last = mm3(bank[1][:, E * t:E * (t + 1)], lambda j: hcur[:, j, 128 * t:128 * (t + 1)],
                               lambda j: gw[:, j, :])
                last.then_inc(s_rp, 1)

            def values_and_mlp(b, norm):
                for n in range(4):
                    if n >= 2:
                        wait(pe, s_v, 4 * b + n - 1)
                    t, q = n // 2, n % 2
                    at = 2 * H * D + 512 * q
                    mm3(bank[2 + n % 2][:, :], lambda j: hcur[:, j, 128 * t:128 * (t + 1)],
                        lambda j: wqkv[:, j, at:at + 512]).then_inc(s_vp, 1)

                def hidden(c):
                    k, m, n, w = CHUNKS[c]
                    if c == FIRST[k]:
                        wait(pe, s_x[k], 16 * 2 * PPB * (b + 1))
                    if c >= 2:
                        wait(pe, s_g, NCH * b + c - 1)
                    for par in range(2):
                        v = rows(X[k][:, par * PPB * SLOT[k]:(par + 1) * PPB * SLOT[k]], SLOT[k])[:, m:m + n, W[k] - w:W[k]]
                        o = rows(bank[4 + c % 2][:, par * n * w:(par + 1) * n * w], w)
                        for j in range(2):
                            mm(o, w1s[:, j, :], v, start=(par == 0 and j == 0), stop=False, skip_group_check=True)
                    t = hk[:, :, :, L - w:L]
                    for j in range(2):
                        for i in range(n):
                            o = bank[4 + c % 2][:, 0:2 * n * w].rearrange("p (a m t) -> p a m t", a=2, m=n)[:, :, i, :]
                            last = mm(o, identh[:, :], t[:, j, :, :], start=False, stop=(j == 1 and i == n - 1), skip_group_check=True)
                    last.then_inc(s_h, 1)

                def logits(c):
                    k, m, n, w = CHUNKS[c]
                    if c >= 2:
                        wait(pe, s_m, NCH * b + c - 1)
                    for par in range(2):
                        v = rows(X[k][:, par * PPB * SLOT[k]:(par + 1) * PPB * SLOT[k]], SLOT[k])[:, m:m + n, W[k] - w:W[k]]
                        mm(rows(bank[6 + c % 2][64 * par:64 * par + 64, 0:n * w], w), sel[:, :], v, stop=False)
                    wait(pe, s_g, NCH * b + c + 1)
                    for par in range(2):
                        last = mm(bank[6 + c % 2][64 * par:64 * par + 64, 0:n * w], w2d[:, :],
                                  Hs[:, c % 2, par * n * w:(par + 1) * n * w], start=False)
                    last.then_inc(s_l, 1)

                hidden(0)
                for c in range(NCH):
                    if c + 1 < NCH:
                        hidden(c + 1)
                    logits(c)
                    if norm and c == NORM_AT:
                        second_transposes(b - 1)
                    if norm and c == ROUTE_AT:
                        route(b - 1)

            pe.wait_ge(s_gd, B)
            pe.wait_ge(s_rot, 4)
            pe.wait_ge(s_zero, 6)
            proj_and_scores(0)
            pe.wait_ge(s_l0, NPAIR)
            pe.wait_ge(s_l1, NPAIR)
            values_and_mlp(0, False)
            with pe.Fori(1, B) as b:
                proj_and_scores(b)
                finish_attention(b - 1, b + 1)
                values_and_mlp(b, True)
            finish_attention(B - 1, B)
            second_transposes(B - 1)
            route(B - 1)

            pe.wait_ge(s_ones, 1)
            pe.wait_ge(s_dr, ROUTER_STEPS)
            mm(bank[7][:, 0:2 * E], ones, tot[:, 0:2 * E]).then_inc(s_tp, 1)

            def experts(g):
                wait(pe, s_mc, g + 1)
                for t in range(4):
                    last = pe.transpose(bank[5][:, :].bitcast(bf16)[0:E, 128 * t:128 * (t + 1)], mcur[:, E * t:E * (t + 1)], identb)
                last.then_inc(s_mtp, 1)
                for m in range(5):
                    if m >= 2 or not isinstance(g, int):
                        wait(pe, s_si, g * 5 + m - 1)
                    mm3(bank[m % 2][:, :], lambda j: ew[:, j, 128 * m:128 * (m + 1)], lambda j: hT[:, j, ds(g * 512, 512)]).then_inc(s_gp, 1)
                    if m >= 2 or not isinstance(g, int):
                        wait(pe, s_a1, g * 5 + m - 1)
                    mm3(bank[2 + m % 2][:, :], lambda j: ew[:, j, NG + 128 * m:NG + 128 * (m + 1)], lambda j: hT[:, j, ds(g * 512, 512)]).then_inc(s_up, 1)
                    if m < 4:
                        if m == 0:
                            wait(pe, s_mt, g + 1)
                        wait(pe, s_a2, g * 4 + m)
                        mm(bank[4][:, :], pickb[:, 128 * m:128 * (m + 1)], mT).then_inc(s_mb, 1)
                wait(pe, s_a2, g * 4 + 4)
                wait(pe, s_a1, g * 5 + 5)
                if isinstance(g, int):
                    pe.wait_ge(s_wm, 1)
                wait(pe, s_r1, g)
                for t in range(4):
                    for m in range(5):
                        last = mm(bank[6][:, HID * t:HID * (t + 1)], acts[:, m, 128 * t:128 * (t + 1)], dn[:, m, :],
                                  start=(m == 0), stop=(m == 4))
                last.then_inc(s_dp, 1)
            pe.wait_ge(s_el, 1)
            experts(0)
            with pe.Fori(1, NT // 4) as g:
                experts(g)


def kernel(**inputs):
    import concourse.bacc as bacc
    from concourse.bass_utils import run_bass_kernel_spmd

    v = {k.removeprefix("L0_"): np.asarray(x) for k, x in inputs.items()}
    arrays = {
        "x": v["attn_x"].reshape(B * L, HID), "wqkv": v["attn_w_qkv"], "wo": v["attn_w_o"],
        "w1": v["attn_w1"], "w2": v["attn_w2"],
        "b1": np.tile(v["attn_b1"], RI)[:, None], "b2": np.tile(v["attn_b2"], 2 * RI)[:, None],
        "pa": np.stack([np.tile(v["attn_log_p"].reshape(-1), 8), np.tile(v["attn_log_a"].reshape(-1), 8)], 1),
        "cT": v["c"].T, "wmod": v["wmod"],
        "egT": v["ffn_expert_gate_w"].reshape(E * I, HID).T, "euT": v["ffn_expert_up_w"].reshape(E * I, HID).T,
        "edT": v["ffn_expert_down_w"].transpose(0, 2, 1).reshape(E * I, HID),
        "sgT": v["ffn_shared_gate_w"].T, "suT": v["ffn_shared_up_w"].T, "sdT": v["ffn_shared_down_w"].T,
        "gwT": v["ffn_gate_w"].T, "lbb": np.tile(v["ffn_lb_bias"], (128, NT)),
    }
    arrays.update(shape_constants())
    arrays = {k: np.ascontiguousarray(x) for k, x in arrays.items()}
    nc = bacc.Bacc("TRN2", target_bir_lowering=False, num_devices=1)
    a = {k: nc.dram_tensor(f"in_{k}", x.shape, mybir.dt.from_np(x.dtype), kind="ExternalInput").ap() for k, x in arrays.items()}
    out = nc.dram_tensor("out_0", (B * L, HID), mybir.dt.float32, kind="ExternalOutput").ap()
    build(nc, a, out)
    r = run_bass_kernel_spmd(nc, [{f"in_{k}": x for k, x in arrays.items()}], core_ids=[0])
    return r.results[0]["out_0"].reshape(B, L, HID)
```

```python
import numpy as np
import concourse.bass as bass
from concourse import mybir
from contextlib import ExitStack

B, L, HID, H, D = 16, 256, 128, 16, 64
TT = L // 128
NT = B * TT
NPAIR = H // 2
E, I, TOPK = 8, 64, 2
HC = 2 * H
RI = 4
RP = 2 * RI
NP = L // RP
NB = 8
PPB = NP // NB
W = [32 * (k + 1) for k in range(NB)]
LEAD = RP * (PPB - 1)
SLACK = RP
SLOT = [w + SLACK for w in W]
CHUNKS = []
for k in reversed(range(NB)):
    n = max(1, min(PPB, L // W[k]))
    for a in range(0, PPB, n):
        CHUNKS.append((k, a, n, W[k] if n > 1 else RP * (PPB * k + a + 1)))
NCH = len(CHUNKS)
NGRP = NP // 4 + NP // 8
SCALE = D ** -0.5
WS = 64.0
EPS_LN, EPS_TOP, FAR = 1e-5, 1e-8, -1e30
MODC, KERPLE, P_FREE = 9, 10, 19
MASK_STEPS = 18
ROUTER_STEPS = 25
DVE_Q = (0, 7)
RA = 3 * NPAIR - len(DVE_Q)


def adds_before(c):
    return 3 * c - sum(q < c for q in DVE_Q)


def row_pair_keys(p):
    return RP * (p + 1)


def shape_constants():
    f = np.float32
    inv = (f(1.0) / f(10000.0) ** (np.arange(0, D, 2, dtype=f) / f(D))).astype(f)
    ang = np.outer(np.arange(L, dtype=f), inv).astype(f)
    emb = np.concatenate([ang, ang], 1)
    cos, sin = np.cos(emb).T.astype(f), np.sin(emb).T.astype(f)
    sin[: D // 2] *= -1
    rope = np.concatenate([np.tile(cos, (2, 1)), np.tile(sin, (2, 1))], 1) / f(WS)
    row = (np.arange(128) // 64) * RI + (np.arange(128) % 64) // H
    at = np.arange(L + SLACK)[None, :] - (L - RP)
    pick = np.zeros((E, E // 2, 128), f)
    for m in range(E // 2):
        pick[2 * m, m, :64] = 1
        pick[2 * m + 1, m, 64:] = 1
    sel = np.zeros((RI, 2, H, RI, H), f)
    for i in range(RI):
        sel[i, :, np.arange(H), i, np.arange(H)] = 1
    return {
        "k_ident": np.eye(128, dtype=f), "k_rope": rope.astype(f), "k_sel": sel.reshape(128, 64),
        "k_future": np.where(at[:, :L] > row[:, None], f(FAR), f(0)).astype(f),
        "k_dist": np.abs(row[:, None] - at).astype(f), "k_pick": pick.reshape(E, -1),
        "k_rank": np.tile(E - np.arange(E, dtype=f), (128, NT)).astype(f),
    }


def build(nc, a, out):
    f32, bf16, f16 = mybir.dt.float32, mybir.dt.bfloat16, mybir.dt.float16
    ALU, ACT, AX = mybir.AluOpType, mybir.ActivationFunctionType, mybir.AxisListType
    ds = bass.ds
    ctx = ExitStack()

    def sb(name, shape, dt=f32):
        return ctx.enter_context(nc.sbuf_tensor(name, shape, dt))

    def sem(name):
        return ctx.enter_context(nc.semaphore(name))

    def wait(eng, s, v):
        if not (isinstance(v, int) and v <= 0):
            eng.wait_ge(s, v)

    with ctx:
        ident, identh = sb("ident", [128, 128]), sb("identh", [128, 128], f16)
        rope = sb("rope", [128, 2 * L])
        logadd = sb("logadd", [128, L])
        wqkv = sb("wqkv", [128, 2, 3 * H * D], f16)
        wrot = sb("wrot", [128, 2, 2 * H * D], f16)
        wo = sb("wo", [128, NPAIR, HID])
        w1s, w2d = sb("w1s", [128, 2, 128], f16), sb("w2d", [128, 64])
        sel = sb("sel", [128, 64], f16)
        hk = sb("hk", [128, 2, 2, L + SLACK], f16)
        hkf = sb("hkf", [128, 2, L + SLACK])
        b1c, b2c, pac = sb("b1c", [128, 1]), sb("b2c", [128, 1]), sb("pac", [128, 12])
        cT = sb("cT", [128, 4, B])
        modc = sb("modc", [128, 4, B + 1])
        wg, cbc = sb("wg", [128, 2 * HID]), sb("cbc", [128, 128])
        gcur, gb = sb("gcur", [128, 2 * HID]), sb("gb", [128, B, HID])
        xall = sb("xall", [128, NT + TT, HID])
        hT = sb("hT", [128, 2, B * L], f16)
        tmax, half = sb("tmax", [128, NT]), sb("half", [128, NT])
        xn, h32 = sb("xn", [128, TT, HID]), sb("h32", [128, L])
        hcur = sb("hcur", [128, 2, L], f16)
        x1 = sb("x1", [128, TT, HID])
        qT, kz = sb("qT", [128, 2, L]), sb("kz", [128, 2, 2, L])
        tmp = sb("tmp", [128, 4, 2 * L])
        V = sb("V", [128, TT, H * D])
        S0, S1 = sb("S0", [128, 2, H, 128], f16), sb("S1", [128, 2, H, L], f16)
        X = [sb(f"X{k}", [128, 2 * PPB * SLOT[k]], f16) for k in range(NB)]
        Hs = sb("Hs", [128, 3, 512])
        P0, P1 = sb("P0", [128, NP // 2, 128]), sb("P1", [128, NP // 2, L])
        warmed = sb("warmed", [128, 1])
        mx, rs, rr = sb("mx", [128, NP]), sb("rs", [128, NP]), sb("rr", [128, NP])
        PT0, PT1 = sb("PT0", [128, H, L]), sb("PT1", [128, H, 128])
        OT = sb("OT", [128, 4, L])
        const = sb("const", [128, 2, TT])
        bna, bnc = sb("bna", [128, TT, 6]), sb("bnc", [128, TT, 6])
        st1, st2 = sb("st1", [128, 2, TT]), sb("st2", [128, 2, TT])
        rlog = sb("rlog", [128, NT * E])
        gw = sb("gw", [128, 2, E], f16)
        top1, top2 = sb("top1", [128, NT]), sb("top2", [128, NT])
        tot, wm = sb("tot", [128, 4 * E]), sb("wm", [128, 4])

        def flat(t):
            return t[:, :, :].rearrange("p a b -> p (a b)")
        PT1f, P0f, P1f, PT0f = flat(PT1), flat(P0), flat(P1), flat(PT0)
        wraw, gwraw = PT0f[:, 0:3 * H * D], P0f[:, 0:E]
        kdist, w1k, w1raw, selraw = P1f[:, 0:L + SLACK], P1f[:, 512:640], P1f[:, 640:768], P1f[:, 768:832]
        rraw = P1f[:, 2048:4096]
        NG = (E + 2) * I
        S1f = S1[:, :, :, :].rearrange("p s h l -> p (s h l)").bitcast(f32)
        wmod = S1f[:, 0:6 * HID]
        eraw = S1f[:, 2048:2048 + 2 * NG]
        ew = wrot[:, :, 0:2 * NG]
        wf = wqkv[:, :, :].rearrange("p s n -> p (s n)").bitcast(f32)
        dn = wf[:, 0:5 * HID].rearrange("p (m n) -> p m n", n=HID)
        lbb, ones, rank, pickraw = wf[:, 768:1024], wf[:, 1024:1152], wf[:, 1152:1408], wf[0:E, 1408:1920]
        rt = PT1f.rearrange("p (k n) -> p k n", n=NT * E)
        Vb = V[:, 1, :].bitcast(bf16)
        maskb = Vb[:, 0:NT * E]
        mT = S0[:, :, :, :].rearrange("p s h l -> p (s h l)").bitcast(bf16)[0:E, :]
        pickb, identb = Vb[0:E, 1024:1536], Vb[:, 1536:1664]
        acts = [f[:, 0:5 * 512].rearrange("p (m n) -> p m n", n=512) for f in (P1f, PT0f)]
        sil = P0f[:, 0:1024].rearrange("p (m n) -> p m n", n=512)
        res = P0f[:, 1024:2048].rearrange("p (m n) -> p m n", n=512)

        bank = [ctx.enter_context(nc.psum_tensor(f"bank{n}", [128, 512], f32)) for n in range(8)]
        four = [bank[n] for n in (0, 1, 4, 5)]
        hbank = [bank[n] for n in (4, 5, 2)]
        other = [bank[n] for n in (2, 3, 6, 7)]

        s_in = [sem(f"s_in{n}") for n in range(6)]
        s_zero = sem("s_zero")
        s_w12 = sem("s_w12")
        s_act0, s_dve0, s_pe0 = sem("s_act0"), sem("s_dve0"), sem("s_pe0")
        s_hi, s_wl = sem("s_hi"), sem("s_wl")
        s_cb, s_gt, s_gd = sem("s_cb"), sem("s_gt"), sem("s_gd")
        s_bn, s_ns, s_pw, s_xn = sem("s_bn"), sem("s_ns"), sem("s_pw"), sem("s_xn")
        s_tr, s_md, s_hh, s_ht = sem("s_tr"), sem("s_md"), sem("s_hh"), sem("s_ht")
        s_hc = sem("s_hc")
        s_qk, s_rm, s_ra = sem("s_qk"), sem("s_rm"), sem("s_ra")
        s_sc, s_sh, s_l0, s_l1 = sem("s_sc"), sem("s_sh"), sem("s_l0"), sem("s_l1")
        s_x = [sem(f"s_rows{k}") for k in range(NB)]
        s_vp, s_v = sem("s_vp"), sem("s_v")
        s_gw = sem("s_gw")
        s_rq = sem("s_rq")
        s_hs = sem("s_hs")
        s_h, s_g, s_l, s_m = sem("s_h"), sem("s_g"), sem("s_l"), sem("s_m")
        s_nm, s_e, s_rc, s_n = sem("s_nm"), sem("s_e"), sem("s_rc"), sem("s_n")
        s_t, s_td, s_ta = sem("s_t"), sem("s_td"), sem("s_ta")
        s_pv, s_o, s_yp, s_y, s_x1 = sem("s_pv"), sem("s_o"), sem("s_yp"), sem("s_y"), sem("s_x1")
        s_xs, s_b2, s_ns2, s_pw2, s_xn2 = sem("s_xs"), sem("s_b2"), sem("s_ns2"), sem("s_pw2"), sem("s_xn2")
        s_tr2, s_md2, s_hh2, s_hl2, s_rp, s_rl = (sem(n) for n in ("s_tr2", "s_md2", "s_hh2", "s_hl2", "s_rp", "s_rl"))
        s_ones = sem("s_ones")
        s_seen2 = sem("s_seen2")
        s_na = sem("s_na")
        s_gs = sem("s_gs")
        s_seen = sem("s_seen")
        s_inm, s_ine = sem("s_inm"), sem("s_ine")
        s_eh, s_el = sem("s_eh"), sem("s_el")
        s_dr, s_al, s_tp, s_wm = sem("s_dr"), sem("s_al"), sem("s_tp"), sem("s_wm")
        s_mtp, s_mt, s_mb = sem("s_mtp"), sem("s_mt"), sem("s_mb")
        s_gp, s_up, s_si, s_a1, s_a2 = sem("s_gp"), sem("s_up"), sem("s_si"), sem("s_a1"), sem("s_a2")
        s_dp, s_r1, s_r2, s_out = sem("s_dp"), sem("s_r1"), sem("s_r2"), sem("s_out")

        def p_slot(p):
            return P0[:, p, :] if p < NP // 2 else P1[:, p - NP // 2, :]

        def pt_view(g):
            dst, q = (PT0, g) if g < NP // 4 else (PT1, g - NP // 4)
            return dst[:, :, 32 * q:32 * q + 32].rearrange("p h i -> p i h")

        def rows(t, n):
            return t.rearrange("p (a n) -> p a n", n=n)

        block = ctx.enter_context(nc.Block())
        FIRST = [min(c for c in range(NCH) if CHUNKS[c][0] == k) for k in range(NB)]
        NPROJ, NSC = 2 * NPAIR, 2 * NPAIR
        HG = NGRP // 2
        NORM_AT, MOD_AT, ROUTE_AT = 6, 9, 15
        ACT_AT = NPAIR - 2
        POOL_BLOCKS = (6, 3)
        DVE_ADDS = [c for c in range(NCH) if c % 4 and c != NORM_AT]
        GATE_AT = 3
        FIRST_AT = 13

        def move_block(eng, k):
            src = S0 if k < NB // 2 else S1
            for par in range(2):
                for m in range(PPB):
                    row = 32 * (k % (NB // 2)) + RP * m + RI * par
                    at = (par * PPB + m) * SLOT[k] + LEAD - RP * m
                    eng.dma_start(X[k][:, at:at + W[k]], src[row:row + RI, :, :, 0:W[k]]).then_inc(s_x[k], 16)

        @block.sync
        def _(sp):
            def x_rows(lo, hi):
                return a["x"][128 * lo:128 * hi, :].rearrange("(t p) n -> p t n", p=128)
            sp.dma_start(xall[:, 0:TT, :], x_rows(0, TT)).then_inc(s_in[5], 16)
            for dst, src in ((cT[:, 0, :], "cT"), (pac[:, 0:2], "pa"), (kdist, "k_dist"), (wmod, "wmod"),
                             (ident[:, :], "k_ident"), (selraw, "k_sel")):
                sp.dma_start(dst, a[src]).then_inc(s_in[0], 16)
            for dst, src in ((wraw, "wqkv"), (rraw, "wrot"), (rope[:, :], "k_rope")):
                sp.dma_start(dst, a[src]).then_inc(s_in[2], 16)
            sp.dma_start(gwraw, a["gwT"]).then_inc(s_in[4], 16)
            sp.wait_ge(s_zero, 3)
            for i in range(RI):
                c = slice(HC * i, HC * (i + 1))
                for j in range(2):
                    sp.dma_start(w1raw[HC * i + H * j:HC * i + H * (j + 1), c], a["w1"][0:H, :]).then_inc(s_w12, 16)
                    sp.dma_start(w1k[64 * j + H * i:64 * j + H * (i + 1), c], a["w1"][H:HC, :]).then_inc(s_w12, 16)
                sp.dma_start(w2d[c, H * i:H * (i + 1)], a["w2"]).then_inc(s_w12, 16)
            for dst, src in ((logadd[:, :], "k_future"), (b1c[:, :], "b1"), (b2c[:, :], "b2")):
                sp.dma_start(dst, a[src]).then_inc(s_in[3], 16)
            sp.dma_start(wo[:, :, :], a["wo"].rearrange("(c p) n -> p c n", p=128)).then_inc(s_in[3], 16)
            sp.dma_start(xall[:, TT:NT, :], x_rows(TT, NT)).then_inc(s_in[1], 16)

            def move_scores(b):
                sp.wait_ge(s_zero, 6 + NB)
                wait(sp, s_l1, NPAIR * (b + 1))
                for k in reversed(range(NB)):
                    if k == NB // 2 - 1:
                        wait(sp, s_l0, NPAIR * (b + 1))
                    if k not in POOL_BLOCKS:
                        move_block(sp, k)

            move_scores(0)
            with sp.Fori(1, B) as b:
                move_scores(b)
            sp.wait_ge(s_vp, 4 * B)
            for dst, src in ((lbb, "lbb"), (rank, "k_rank"), (pickraw, "k_pick"), (dn[:, 4, :], "sdT")):
                sp.dma_start(dst, a[src]).then_inc(s_inm, 16)
            sp.dma_start(dn[:, 0:4, :], a["edT"].rearrange("(m p) n -> p m n", p=128)).then_inc(s_inm, 16)
            for k in range(NB):
                sp.wait_ge(s_x[k], 16 * 2 * PPB * B)
            at = 0
            for src in ("egT", "sgT", "euT", "suT"):
                n = a[src].shape[1]
                sp.dma_start(eraw[:, at:at + n], a[src]).then_inc(s_ine, 16)
                at += n

            def store(g, u):
                sp.wait_ge(s_r2, g + u + 1)
                sp.dma_start(out[ds((g + u) * 512, 512), :].rearrange("(t p) n -> p t n", p=128),
                             rows(res[:, u, :], HID)).then_inc(s_out, 16)
            with sp.Fori(0, NT // 8) as r2:
                for u in range(2):
                    store(r2 * 2, u)
            sp.wait_ge(s_out, 16 * (NT // 4))

        @block.gpsimd
        def _(pool):
            def rstd(st, dst, steps, b):
                me, ve, mo, vo = (st[:, :, j] for j in (1, 2, 4, 5))
                k = [0]

                def part(o, i, j, op):
                    k[0] += 1
                    pool.tensor_tensor(o, i, j, op).then_inc(steps, 1)
                    wait(pool, steps, 8 * b + k[0])
                part(dst[:, 0, :], me, mo, ALU.add)
                part(me, me, mo, ALU.subtract)
                part(me, me, half[:, 0:TT], ALU.mult)
                part(me, me, me, ALU.mult)
                part(ve, ve, vo, ALU.add)
                part(ve, ve, const[:, 0, :], ALU.mult)
                part(ve, ve, me, ALU.add)
                part(ve, ve, const[:, 1, :], ALU.add)
                pool.tensor_tensor(dst[:, 0, :], dst[:, 0, :], half[:, 0:TT], ALU.mult)
                return pool.tensor_tensor(dst[:, 1, :], ve, half[:, 0:TT], ALU.pow)

            def first_rstd(b):
                wait(pool, s_bn, TT * (b + 1))
                rstd(bna, st1, s_ns, b).then_inc(s_pw, 1)

            pool.memset(w1raw, 0.0).then_inc(s_zero, 1)
            pool.memset(w1k, 0.0).then_inc(s_zero, 1)
            pool.memset(w2d[:, :], 0.0).then_inc(s_zero, 1)
            pool.memset(const[:, 0, :], 1 / HID)
            pool.memset(const[:, 1, :], EPS_LN)
            pool.memset(half[:, :], -0.5).then_inc(s_zero, 1)
            pool.memset(kz[:, :, :, :], 0.0).then_inc(s_zero, 1)
            pool.memset(xall[:, NT:, :], 0.0).then_inc(s_zero, 1)
            for k in range(NB):
                pool.memset(X[k][:, :], 0.0).then_inc(s_zero, 1)
            pool.wait_ge(s_zero, 4)
            first_rstd(0)
            pool.wait_ge(s_dve0, P_FREE)
            pool.wait_ge(s_wl, 2)
            pool.memset(P0[:, :, :], 0.0).then_inc(s_zero, 1)
            pool.memset(P1[:, :, :], 0.0).then_inc(s_zero, 1)

            def rope_adds(b):
                for n in range(NPROJ):
                    c, u = n // 2, n // 2 % 2
                    wait(pool, s_rm, NPROJ * b + n + 1)
                    t = tmp[:, n % 4, :]
                    if n % 2 == 0:
                        if c >= 2 or not isinstance(b, int):
                            wait(pool, s_sc, NSC * b + 2 * max(c - 1, 0))
                        wait(pool, s_ra, RA * b + adds_before(c))
                        if c not in DVE_Q:
                            pool.tensor_tensor(qT[:, u, :], t[:, 0:L], t[:, L:2 * L], ALU.add).then_inc(s_ra, 1)
                    else:
                        for e in range(2):
                            r = slice(64 * e, 64 * e + 64)
                            wait(pool, s_ra, RA * b + adds_before(c + 1) - 2 + e)
                            pool.tensor_tensor(kz[r, u, e, :], t[r, 0:L], t[r, L:2 * L], ALU.add).then_inc(s_ra, 1)

            def second_norm(b):
                wait(pool, s_x1, b + 1)
                pool.tensor_copy(xall[:, ds(b * TT, TT), :], x1[:, :, :]).then_inc(s_xs, 1)
                wait(pool, s_b2, TT * (b + 1))
                rstd(bnc, st2, s_ns2, b).then_inc(s_pw2, 1)

            def move_scores(b):
                wait(pool, s_l1, NPAIR * (b + 1))
                pool.sem_inc(s_seen2, 1)
                for k in POOL_BLOCKS:
                    move_block(pool, k)

            rope_adds(0)
            move_scores(0)
            first_rstd(1)
            with pool.Fori(1, B) as b:
                rope_adds(b)
                move_scores(b)
                second_norm(b - 1)
                first_rstd(b + 1)
            second_norm(B - 1)
            pool.wait_ge(s_vp, 4 * B)
            pool.memset(ones, 1.0).then_inc(s_ones, 1)

        @block.scalar
        def _(act):
            act.wait_ge(s_in[0], 96)
            act.activation(cT[:, 1, :], cT[:, 0, :], ACT.Exp, scale=-1.0).then_inc(s_act0, 1)
            act.wait_ge(s_dve0, 1)
            act.activation(pac[:, 4:6], pac[:, 2:4], ACT.Exp, scale=-1.0).then_inc(s_act0, 1)
            act.wait_ge(s_act0, 2)
            act.activation(pac[:, 6:8], pac[:, 4:6], ACT.Ln, bias=1.0).then_inc(s_act0, 1)
            act.wait_ge(s_dve0, 5)
            act.activation(kdist, kdist, ACT.Ln, scale=pac[:, 9:10], bias=1.0).then_inc(s_act0, 1)
            act.wait_ge(s_in[2], 48)
            act.activation(wqkv[:, 0, :], wraw, ACT.Copy, scale=WS).then_inc(s_hi, 1)
            act.activation(wrot[:, 0, :], rraw, ACT.Copy, scale=WS).then_inc(s_hi, 1)
            act.wait_ge(s_in[4], 16)
            act.activation(gw[:, 0, :], gwraw, ACT.Copy, scale=WS).then_inc(s_hi, 1)

            def first_modulate(b):
                wait(act, s_tr, b + 1)
                if not isinstance(b, int) or b >= 2:
                    wait(act, s_ht, b - 1)
                act.activation(h32[:, :], bank[3][:, 0:L], ACT.Identity,
                               scale=modc[:, 1, ds(b, 1)], bias=modc[:, 0, ds(b, 1)]).then_inc(s_md, 1)
            act.wait_ge(s_dve0, MODC)
            act.wait_ge(s_zero, 4)
            first_modulate(0)

            def score_highs(b, c):
                wait(act, s_sc, NSC * b + 2 * c + 1)
                if c == 0:
                    for k in range(NB):
                        wait(act, s_x[k], 16 * 2 * PPB * b)
                act.activation(S0[:, 0, 2 * c:2 * c + 2, :], rows(bank[(2, 6)[c % 2]][:, 0:256], 128), ACT.Copy, scale=SCALE).then_inc(s_sh, 1)
                wait(act, s_sc, NSC * b + 2 * c + 2)
                act.activation(S1[:, 0, 2 * c:2 * c + 2, :], rows(bank[(3, 7)[c % 2]][:, :], L), ACT.Copy, scale=SCALE).then_inc(s_sh, 1)

            def exps(b, c):
                if c == 0:
                    wait(act, s_nm, b + 1)
                for p in range(4 * c, 4 * c + 4):
                    w = row_pair_keys(p)
                    act.activation(p_slot(p)[:, 0:w], p_slot(p)[:, 0:w], ACT.Exp, bias=mx[:, p:p + 1],
                                   accum_out=rs[:, p:p + 1]).then_inc(s_e, 1)

            def copy_transposed(b, g):
                wait(act, s_t, NGRP * b + g + 1)
                act.activation(pt_view(g), rows(four[g % 4][:, :], H), ACT.Copy).then_inc(s_ta, 1)

            def normalise(b, c):
                wait(act, s_rc, NPAIR * b + c + 1)
                for p in range(4 * c, 4 * c + 4):
                    w = row_pair_keys(p)
                    ins = act.activation(p_slot(p)[:, 0:w], p_slot(p)[:, 0:w], ACT.Copy, scale=rr[:, p:p + 1])
                ins.then_inc(s_na, 1)

            def warm(func):
                act.activation(warmed[:, :], half[:, 0:1], func)

            def finish_attention(b):
                for g in range(3, NGRP, 2):
                    copy_transposed(b, g)
                for c in range(NPAIR):
                    if c >= 4:
                        wait(act, s_yp, NPAIR * b + c - 3)
                    wait(act, s_pv, NPAIR * b + c + 1)
                    act.activation(OT[:, c % 4, :], other[c % 4][:, 0:L], ACT.Copy).then_inc(s_o, 1)
                    if c == 3:
                        warm(ACT.Gelu)

            def second_modulate(b):
                wait(act, s_tr2, b + 1)
                act.activation(h32[:, :], bank[0][:, 0:L], ACT.Identity,
                               scale=modc[:, 3, ds(b, 1)], bias=modc[:, 2, ds(b, 1)]).then_inc(s_md2, 1)

            def mlp_side(b, norm):
                for n in range(4):
                    wait(act, s_vp, 4 * b + n + 1)
                    act.activation(V[:, n // 2, 512 * (n % 2):512 * (n % 2) + 512], bank[2 + n % 2][:, :], ACT.Copy, scale=1 / WS).then_inc(s_v, 1)
                for c, (k, m, n, w) in enumerate(CHUNKS):
                    N = 2 * n * w
                    if c >= 3:
                        wait(act, s_l, NCH * b + c - 2)
                    if c in DVE_ADDS:
                        wait(act, s_hs, len(DVE_ADDS) * b + DVE_ADDS.index(c) + 1)
                        src = Hs[:, c % 3, 0:N]
                    else:
                        wait(act, s_h, NCH * b + c + 1)
                        src = hbank[c % 3][:, 0:N]
                    act.activation(Hs[:, c % 3, 0:N], src, ACT.Gelu, bias=b1c[:, :], scale=1 / WS).then_inc(s_g, 1)
                    if norm and c == MOD_AT:
                        second_modulate(b - 1)
                    if c == FIRST_AT + 2:
                        first_modulate(b + 1)

            for c in range(NPAIR):
                score_highs(0, c)
            act.wait_ge(s_in[3], 64)
            mlp_side(0, False)
            with act.Fori(1, B) as b:
                warm(ACT.Exp)
                exps(b - 1, 0)
                exps(b - 1, 1)
                for c in range(NPAIR):
                    score_highs(b, c)
                    if c + 2 < NPAIR:
                        exps(b - 1, c + 2)
                    else:
                        if c == NPAIR - 1:
                            copy_transposed(b - 1, 1)
                        normalise(b - 1, c)
                finish_attention(b - 1)
                mlp_side(b, True)
            for c in range(NPAIR):
                exps(B - 1, c)
            act.wait_ge(s_ine, 64)
            act.activation(ew[:, 0, :], eraw, ACT.Copy, scale=WS).then_inc(s_eh, 1)
            copy_transposed(B - 1, 1)
            finish_attention(B - 1)
            second_modulate(B - 1)

            act.wait_ge(s_dr, 3)
            act.activation(rt[:, 1, :], rlog[:, :], ACT.Exp, scale=-1.0).then_inc(s_al, 1)

            def silus(g, u):
                for m in range(5):
                    if m >= 2 or not isinstance(g, int) or g > 0:
                        wait(act, s_a1, g * 5 + m - 1)
                    wait(act, s_gp, g * 5 + m + 1)
                    act.activation(sil[:, (u + m) % 2, :], bank[(u + m) % 2][:, :], ACT.Silu, scale=1 / WS).then_inc(s_si, 1)
            silus(0, 0)
            silus(1, 1)
            with act.Fori(1, NT // 8) as r2:
                for u in range(2):
                    silus(r2 * 2 + u, u)

        @block.vector
        def _(dve):
            count = [0]

            def step(ins):
                count[0] += 1
                ins.then_inc(s_dve0, 1)
                dve.wait_ge(s_dve0, count[0])

            dve.wait_ge(s_in[0], 96)
            step(dve.scalar_tensor_tensor(pac[:, 2:4], pac[:, 0:2], -1.0, pac[:, 0:2], ALU.mult, ALU.max))
            dve.wait_ge(s_act0, 1)
            step(dve.tensor_scalar(cT[:, 2, :], cT[:, 1, :], 1.0, None, ALU.add))
            step(dve.reciprocal(cT[:, 1, :], cT[:, 2, :]))
            step(dve.tensor_tensor(cT[:, 3, :], cT[:, 0, :], cT[:, 1, :], ALU.mult))
            dve.wait_ge(s_act0, 3)
            step(dve.scalar_tensor_tensor(pac[:, 8:10], pac[:, 0:2], 0.0, pac[:, 6:8], ALU.max, ALU.add))
            step(dve.tensor_scalar(pac[:, 10:11], pac[:, 8:9], -1.0, None, ALU.mult))
            step(dve.tensor_copy(identh[:, :], ident[:, :]))
            step(dve.tensor_copy(sel[:, :], selraw))
            def spread(b):
                dve.tensor_copy(cbc[:, :], cT[:, 3, ds(b, 1)].to_broadcast([128, 128])).then_inc(s_cb, 1)

            def gate(b, part):
                g = bank[3][:, 0:2 * HID]
                if part == 0:
                    wait(dve, s_gt, b + 1)
                    dve.tensor_scalar(h32[:, :], g, 0.0, 2.0, ALU.is_ge, ALU.mult).then_inc(s_gs, 1)
                    dve.tensor_scalar(gcur[:, :], g, -1.0, 0.25, ALU.mult, ALU.max).then_inc(s_gs, 1)
                if part == 1:
                    wait(dve, s_gs, 3 * b + 2)
                    dve.tensor_tensor(gcur[:, :], gcur[:, :], g, ALU.max).then_inc(s_gs, 1)
                if part == 2:
                    wait(dve, s_gs, 3 * b + 3)
                    dve.scalar_tensor_tensor(gb[:, ds(b, 1), :].rearrange("p a n -> p (a n)"), h32[:, HID:], -1.0, gcur[:, HID:], ALU.add, ALU.mult)
                    dve.scalar_tensor_tensor(gcur[:, 0:HID], h32[:, 0:HID], -1.0, gcur[:, 0:HID], ALU.add, ALU.mult).then_inc(s_gd, 1)

            def first_stats(b):
                for t in range(TT):
                    dve.bn_stats(bna[:, t, :], xall[:, ds(b * TT + t, 1), :].rearrange("p a n -> p (a n)")).then_inc(s_bn, 1)

            def first_rows(b):
                wait(dve, s_pw, b + 1)
                if not isinstance(b, int) or b >= 2:
                    wait(dve, s_tr2, b - 1)
                for t in range(TT):
                    ins = dve.tensor_scalar(xn[:, t, :], xall[:, ds(b * TT + t, 1), :].rearrange("p a n -> p (a n)"),
                                            st1[:, 0, t:t + 1], st1[:, 1, t:t + 1], ALU.add, ALU.mult)
                ins.then_inc(s_xn, 1)

            def first_parts(b):
                wait(dve, s_md, b + 1)
                dve.tensor_copy(hcur[:, 0, :], h32[:, :]).then_inc(s_hh, 1)
                wait(dve, s_hh, b + 1)
                dve.tensor_tensor(hcur[:, 1, :], h32[:, :], hcur[:, 0, :], ALU.subtract).then_inc(s_hc, 1)

            dve.wait_ge(s_in[5], 16)
            first_stats(0)
            dve.memset(modc[:, :, B:], 0.0)
            dve.tensor_copy(wg[:, 0:HID], wmod[:, 2 * HID:3 * HID])
            dve.tensor_copy(wg[:, HID:], wmod[:, 5 * HID:])
            dve.wait_ge(s_pe0, 1)
            for j in range(4):
                last = dve.tensor_scalar(modc[:, j, 0:B], bank[2][:, B * j:B * (j + 1)], float(j % 2), None, ALU.add)
            step(last)
            assert count[0] == MODC
            dve.wait_ge(s_act0, 4)
            step(dve.tensor_scalar(kdist, kdist, pac[:, 10:11], None, ALU.mult))
            assert count[0] == KERPLE
            first_rows(0)
            dve.wait_ge(s_hi, 1)
            dve.scalar_tensor_tensor(wqkv[:, 1, :], wraw, WS, wqkv[:, 0, :], ALU.mult, ALU.subtract).then_inc(s_wl, 1)
            dve.wait_ge(s_hi, 2)
            dve.scalar_tensor_tensor(wrot[:, 1, :], rraw, WS, wrot[:, 0, :], ALU.mult, ALU.subtract).then_inc(s_wl, 1)
            first_parts(0)
            dve.wait_ge(s_hi, 3)
            dve.scalar_tensor_tensor(gw[:, 1, :], gwraw, WS, gw[:, 0, :], ALU.mult, ALU.subtract).then_inc(s_gw, 1)
            dve.wait_ge(s_in[3], 64)
            step(dve.scalar_tensor_tensor(logadd[:, :], logadd[:, :], b2c[:, :], kdist[:, 0:L], ALU.add, ALU.add))
            dve.wait_ge(s_w12, 16 * 5 * RI)
            step(dve.tensor_scalar(w1s[:, 0, :], w1raw, WS, None, ALU.mult))
            step(dve.scalar_tensor_tensor(w1s[:, 1, :], w1raw, WS, w1s[:, 0, :], ALU.mult, ALU.subtract))
            dve.wait_ge(s_pe0, 2)
            for par in range(2):
                step(dve.tensor_scalar(hkf[:, par, :], bank[6 + par][:, 0:L + SLACK], WS, None, ALU.mult))
                step(dve.tensor_scalar(hk[:, 0, par, :], bank[6 + par][:, 0:L + SLACK], WS, None, ALU.mult))
                step(dve.scalar_tensor_tensor(hk[:, 1, par, :], bank[6 + par][:, 0:L + SLACK], WS, hk[:, 0, par, :], ALU.mult, ALU.subtract))
            assert count[0] == P_FREE

            def proj_and_scores(b, soft):
                def products(c):
                    for n in (2 * c, 2 * c + 1):
                        if n >= 4 or not isinstance(b, int):
                            before = RA * b + adds_before(c - 2) if c >= 2 else RA * (b - 1) + adds_before(c - 2 + NPAIR)
                            pool_adds = adds_before((c - 2) % NPAIR + 1) - adds_before((c - 2) % NPAIR)
                            if n % 2 == 1 or pool_adds == 3:
                                wait(dve, s_ra, before + (1 if n % 2 == 0 else pool_adds))
                            else:
                                wait(dve, s_rq, len(DVE_Q) * (b if c >= 2 else b - 1) + DVE_Q.index((c - 2) % NPAIR) + 1)
                        wait(dve, s_qk, NPROJ * b + n + 1)
                        dve.tensor_tensor(tmp[:, n % 4, :], four[n % 4][:, :], rope[:, :], ALU.mult).then_inc(s_rm, 1)
                def add_q(c):
                    if c in DVE_Q:
                        wait(dve, s_rm, NPROJ * b + 2 * c + 1)
                        dve.tensor_tensor(qT[:, c % 2, :], tmp[:, 2 * c % 4, 0:L], tmp[:, 2 * c % 4, L:2 * L], ALU.add).then_inc(s_rq, 1)
                products(0)
                products(1)
                add_q(0)
                add_q(1)
                if soft:
                    normalise(b - 1, 0)
                for c in range(NPAIR):
                    if c + 2 < NPAIR:
                        products(c + 2)
                    if soft and c + 1 < NPAIR:
                        normalise(b - 1, c + 1)
                    wait(dve, s_sh, NSC * b + 2 * c + 1)
                    dve.scalar_tensor_tensor(S0[:, 1, 2 * c:2 * c + 2, :], rows(bank[(2, 6)[c % 2]][:, 0:256], 128), SCALE,
                                             S0[:, 0, 2 * c:2 * c + 2, :], ALU.mult, ALU.subtract).then_inc(s_l0, 1)
                    wait(dve, s_sh, NSC * b + 2 * c + 2)
                    dve.scalar_tensor_tensor(S1[:, 1, 2 * c:2 * c + 2, :], rows(bank[(3, 7)[c % 2]][:, :], L), SCALE,
                                             S1[:, 0, 2 * c:2 * c + 2, :], ALU.mult, ALU.subtract).then_inc(s_l1, 1)
                    if c + 2 < NPAIR:
                        add_q(c + 2)
                    if soft and c == NPAIR - 2:
                        copy_transposed(b - 1, 0)
                if soft:
                    copy_transposed(b - 1, 2)

            def copy_transposed(b, g):
                wait(dve, s_t, NGRP * b + g + 1)
                dve.tensor_copy(pt_view(g), rows(four[g % 4][:, :], H)).then_inc(s_td, 1)

            def normalise(b, c, last=False):
                wait(dve, s_e, NP * b + 4 * c + 4)
                dve.reciprocal(rr[:, 4 * c:4 * c + 4], rs[:, 4 * c:4 * c + 4]).then_inc(s_rc, 1)
                if c >= ACT_AT and not last:
                    return
                wait(dve, s_rc, NPAIR * b + c + 1)
                for p in range(4 * c, 4 * c + 4):
                    w = row_pair_keys(p)
                    ins = dve.tensor_scalar(p_slot(p)[:, 0:w], p_slot(p)[:, 0:w], rr[:, p:p + 1], None, ALU.mult)
                ins.then_inc(s_n if c < ACT_AT else s_na, 1)

            def finish_attention(b):
                for g in range(4, NGRP, 2):
                    copy_transposed(b, g)
                wait(dve, s_yp, NPAIR * (b + 1))
                for t in range(TT):
                    ins = dve.tensor_tensor(xn[:, t, :], bank[t][:, 0:HID], gcur[:, 0:HID], ALU.mult)
                ins.then_inc(s_y, 1)
                wait(dve, s_y, b + 1)
                dve.tensor_tensor(x1[:, :, :], xall[:, ds(b * TT, TT), :], xn[:, :, :], ALU.add).then_inc(s_x1, 1)
                wait(dve, s_x1, b + 1)
                for t in range(TT):
                    dve.bn_stats(bnc[:, t, :], x1[:, t, :]).then_inc(s_b2, 1)

            def second_rows(b):
                wait(dve, s_pw2, b + 1)
                for t in range(TT):
                    ins = dve.tensor_scalar(xn[:, t, :], x1[:, t, :], st2[:, 0, t:t + 1], st2[:, 1, t:t + 1], ALU.add, ALU.mult)
                ins.then_inc(s_xn2, 1)

            def second_parts(b):
                wait(dve, s_md2, b + 1)
                dve.tensor_copy(hcur[:, 0, :], h32[:, :]).then_inc(s_hh2, 1)
                wait(dve, s_hh2, b + 1)
                dve.tensor_tensor(hcur[:, 1, :], h32[:, :], hcur[:, 0, :], ALU.subtract).then_inc(s_hl2, 1)
                wait(dve, s_hl2, b + 1)
                dve.tensor_copy(hT[:, :, ds(b * L, L)], hcur[:, :, :]).then_inc(s_ht, 1)

            def second_logits(b):
                wait(dve, s_rp, b + 1)
                dve.tensor_scalar(rlog[:, ds(b * TT * E, TT * E)], bank[1][:, 0:TT * E], 1 / WS, None, ALU.mult).then_inc(s_rl, 1)

            def add_kerple(b, c):
                k, m, n, w = CHUNKS[c]
                wait(dve, s_h, NCH * b + c + 1)
                for par in range(2):
                    at = slice(par * n * w, (par + 1) * n * w)
                    t = hkf[:, par, L - w:L]
                    if n > 1:
                        t = t.unsqueeze(1).to_broadcast([128, n, w])
                    o, i = Hs[:, c % 3, at], hbank[c % 3][:, at]
                    ins = dve.tensor_tensor(rows(o, w) if n > 1 else o, rows(i, w) if n > 1 else i, t, ALU.add)
                ins.then_inc(s_hs, 1)

            def maxima(b, norm):
                spread(b)
                for c in (0, 1):
                    if c in DVE_ADDS:
                        add_kerple(b, c)
                for c, (k, m, n, w) in enumerate(CHUNKS):
                    if c == 0:
                        dve.wait_ge(s_zero, 8 + NB)
                    if c + 2 in DVE_ADDS:
                        add_kerple(b, c + 2)
                    wait(dve, s_l, NCH * b + c + 1)
                    dve.sem_inc(s_seen, 1)
                    for j in range(n):
                        p = PPB * k + m + j
                        e = row_pair_keys(p)
                        ins = dve.tensor_tensor_reduce(out=p_slot(p)[:, 0:e], in0=bank[6 + c % 2][:, j * w + w - e:j * w + w],
                                                       in1=logadd[:, L - e:L], scale=1.0, scalar=3.0 * FAR, op0=ALU.add, op1=ALU.max,
                                                       accum_out=mx[:, p:p + 1])
                    ins.then_inc(s_m, 1)
                    if GATE_AT <= c < GATE_AT + 3:
                        gate(b, c - GATE_AT)
                    if norm and c == NORM_AT - 3:
                        second_rows(b - 1)
                    if c == NORM_AT:
                        first_stats(b + 1)
                    if c == FIRST_AT - 2:
                        first_rows(b + 1)
                    if norm and c == MOD_AT + 1:
                        second_parts(b - 1)
                    if norm and c == ROUTE_AT + 2:
                        second_logits(b - 1)
                    if c == ROUTE_AT + 2:
                        first_parts(b + 1)
                wait(dve, s_m, NCH * (b + 1))
                dve.tensor_scalar(mx[:, :], mx[:, :], -1.0, None, ALU.mult).then_inc(s_nm, 1)

            proj_and_scores(0, False)
            dve.wait_ge(s_in[1], 16)
            maxima(0, False)
            with dve.Fori(1, B) as b:
                proj_and_scores(b, True)
                finish_attention(b - 1)
                maxima(b, True)
            for c in range(NPAIR):
                normalise(B - 1, c, last=True)
            copy_transposed(B - 1, 0)
            copy_transposed(B - 1, 2)
            finish_attention(B - 1)
            dve.wait_ge(s_eh, 1)
            dve.scalar_tensor_tensor(ew[:, 1, :], eraw, WS, ew[:, 0, :], ALU.mult, ALU.subtract).then_inc(s_el, 1)
            second_rows(B - 1)
            second_parts(B - 1)
            second_logits(B - 1)

            dve.wait_ge(s_rl, B)
            dve.wait_ge(s_inm, 80)
            n_ = [0]

            def rstep(ins):
                n_[0] += 1
                ins.then_inc(s_dr, 1)
                dve.wait_ge(s_dr, n_[0])

            def by_e(x):
                return x.rearrange("p (t e) -> p t e", e=E)
            ex, sc_, eq, fi, s2_, mk, wt = (rt[:, j, :] for j in range(1, 8))
            rstep(dve.tensor_copy(identb, ident[:, :]))
            rstep(dve.tensor_copy(pickb, pickraw))
            rstep(dve.tensor_tensor(rlog[:, :], rlog[:, :], lbb, ALU.add))
            dve.wait_ge(s_al, 1)
            rstep(dve.tensor_scalar(ex, ex, 1.0, None, ALU.add))
            rstep(dve.reciprocal(sc_, ex))

            def top(of, dst, m):
                rstep(dve.tensor_reduce(m, by_e(of), AX.X, ALU.max))
                rstep(dve.tensor_tensor(by_e(eq), by_e(of), m.unsqueeze(2).to_broadcast([128, NT, E]), ALU.is_equal))
                rstep(dve.tensor_tensor(eq, eq, rank, ALU.mult))
                rstep(dve.tensor_reduce(tmax[:, :], by_e(eq), AX.X, ALU.max))
                rstep(dve.tensor_tensor(by_e(dst), by_e(eq), tmax[:, :].unsqueeze(2).to_broadcast([128, NT, E]), ALU.is_equal))
            m1, m2 = top1[:, :], top2[:, :]
            top(sc_, fi, m1)
            rstep(dve.scalar_tensor_tensor(s2_, fi, -4.0, sc_, ALU.mult, ALU.add))
            top(s2_, mk, m2)
            rstep(dve.tensor_tensor(mk, mk, fi, ALU.add))
            rstep(dve.tensor_copy(maskb, mk))
            assert n_[0] == MASK_STEPS
            rstep(dve.tensor_tensor(m1, m1, m2, ALU.add))
            rstep(dve.tensor_scalar(m1, m1, EPS_TOP, None, ALU.add))
            rstep(dve.reciprocal(m2, m1))
            rstep(dve.tensor_tensor(wt, mk, sc_, ALU.mult))
            rstep(dve.tensor_tensor(by_e(wt), by_e(wt), m2.unsqueeze(2).to_broadcast([128, NT, E]), ALU.mult))
            rstep(dve.tensor_reduce(tot[:, 0:E], wt.rearrange("p (t e) -> p e t", e=E), AX.X, ALU.add))
            rstep(dve.tensor_reduce(tot[:, E:2 * E], mk.rearrange("p (t e) -> p e t", e=E), AX.X, ALU.add))
            assert n_[0] == ROUTER_STEPS
            for g in range(NT // 4):
                dve.wait_ge(s_mtp, g + 1)
                dve.tensor_copy(mT[:, 512 * g:512 * (g + 1)], bank[g % 7][:, :].bitcast(bf16)[0:E, 0:512]).then_inc(s_mt, 1)
            dve.wait_ge(s_tp, 1)
            rstep(dve.tensor_scalar(tot[:, 2 * E:3 * E], bank[7][:, E:2 * E], 1.0, None, ALU.max))
            rstep(dve.reciprocal(tot[:, 3 * E:4 * E], tot[:, 2 * E:3 * E]))
            rstep(dve.tensor_tensor(tot[:, 0:E], tot[:, 3 * E:4 * E], bank[7][:, 0:E], ALU.mult))
            tv = tot[:, 0:E].rearrange("p (m a) -> p m a", a=2)
            rstep(dve.tensor_copy(wm[0:64, :], tv[0:64, :, 0]))
            rstep(dve.tensor_copy(wm[64:128, :], tv[64:128, :, 1]))
            for m in range(4):
                last = dve.tensor_scalar(dn[:, m, :], dn[:, m, :], wm[:, m:m + 1], None, ALU.mult)
            last.then_inc(s_wm, 1)

            def experts(g, u):
                first = isinstance(g, int) and g == 0
                wait(dve, s_dp, g - 1)
                for m in range(5):
                    wait(dve, s_si, g * 5 + m + 1)
                    wait(dve, s_up, g * 5 + m + 1)
                    dve.scalar_tensor_tensor(acts[u][:, m, :], bank[2 + (u + m) % 2][:, :], 1 / WS, sil[:, (u + m) % 2, :], ALU.mult, ALU.mult).then_inc(s_a1, 1)
                    if m < 4:
                        wait(dve, s_a1, g * 5 + m + 1)
                        wait(dve, s_mb, g * 4 + m + 1)
                        dve.tensor_tensor(acts[u][:, m, :], acts[u][:, m, :], bank[4 + m % 2][:, :], ALU.mult).then_inc(s_a2, 1)
                if not first:
                    result(g - 1, 1 - u)

            def result(g, u):
                wait(dve, s_out, 16 * g)
                wait(dve, s_dp, g + 1)
                for t in range(4):
                    last = dve.tensor_tensor(res[:, u, HID * t:HID * (t + 1)], bank[6 + u][:, HID * t:HID * (t + 1)],
                                             gb[:, ds(2 * g + t // 2, 1), :].rearrange("p a n -> p (a n)"), ALU.mult)
                last.then_inc(s_r1, 1)
                wait(dve, s_r1, g + 1)
                o = rows(res[:, u, :], HID)
                dve.tensor_tensor(o, o, xall[:, ds(g * 4, 4), :], ALU.add).then_inc(s_r2, 1)
            experts(0, 0)
            experts(1, 1)
            with dve.Fori(1, NT // 8) as r2:
                for u in range(2):
                    experts(r2 * 2 + u, u)
            result(NT // 4 - 1, 1)

        @block.tensor
        def _(pe):
            def mm(o, l, r, start=True, stop=True, **kw):
                return pe.matmul(o, l, r, start=start, stop=stop, **kw)

            def mm3(o, l, r):
                mm(o, l(0), r(0), stop=False)
                mm(o, l(0), r(1), start=False, stop=False)
                return mm(o, l(1), r(0), start=False)

            pe.wait_ge(s_in[0], 96)
            pe.wait_ge(s_dve0, 4)
            for j, part in enumerate((0, 1, 3, 4)):
                last = mm(bank[2][:, B * j:B * (j + 1)], wmod[:, HID * part:HID * (part + 1)], cT[:, 3, :])
            last.then_inc(s_pe0, 1)

            def gates_product(b):
                wait(pe, s_cb, b + 1)
                mm(bank[3][:, 0:2 * HID], cbc[:, :], wg[:, :]).then_inc(s_gt, 1)

            def first_transposes(b):
                wait(pe, s_xn, b + 1)
                for t in range(TT):
                    last = pe.transpose(bank[3][:, 128 * t:128 * (t + 1)], xn[:, t, :], ident[:, :])
                last.then_inc(s_tr, 1)
            first_transposes(0)
            pe.wait_ge(s_dve0, KERPLE)
            pe.wait_ge(s_w12, 16 * 5 * RI)
            for par in range(2):
                r = slice(64 * par, 64 * par + 64)
                last = mm(bank[6 + par][:, 0:L + SLACK], w1k[r, :], kdist[r, :])
            last.then_inc(s_pe0, 1)


            def proj(b, n):
                c, base = n // 2, (0, H * D)[n % 2]
                o = four[n % 4]
                if n == 0:
                    wait(pe, s_hc, b + 1)
                if n >= 4:
                    wait(pe, s_rm, NPROJ * b + n - 3)
                at = base + 128 * c
                mm3(o[:, 0:L], lambda j: wqkv[:, j, at:at + 128], lambda j: hcur[:, j, :])
                mm3(o[:, L:2 * L], lambda j: wrot[:, j, at:at + 128], lambda j: hcur[:, j, :]).then_inc(s_qk, 1)

            def scores(b, c):
                u = c % 2
                if c in DVE_Q:
                    wait(pe, s_rq, len(DVE_Q) * b + DVE_Q.index(c) + 1)
                wait(pe, s_ra, RA * b + adds_before(c + 1))
                if c == 0:
                    wait(pe, s_gd, b)
                if c == 1 and isinstance(b, int):
                    pe.wait_ge(s_dve0, P_FREE)
                elif c == 1:
                    wait(pe, s_m, NCH * b)
                if c >= 2:
                    wait(pe, s_l0, NPAIR * b + c - 1)
                mm(rows(bank[(2, 6)[u]][:, 0:256], 128), qT[:, u, 0:128], kz[:, u, :, 0:128]).then_inc(s_sc, 1)
                if c >= 2:
                    wait(pe, s_l1, NPAIR * b + c - 1)
                mm(rows(bank[(3, 7)[u]][:, :], L), qT[:, u, 128:256], kz[:, u, :, :]).then_inc(s_sc, 1)

            def proj_and_scores(b, soft):
                for n in range(4):
                    proj(b, n)
                for c in range(NPAIR):
                    if c + 2 < NPAIR:
                        proj(b, 2 * c + 4)
                        proj(b, 2 * c + 5)
                    scores(b, c)
                    if soft and c >= NPAIR - 2:
                        transpose_weights(b - 1, (0, 1) if c == NPAIR - 2 else (2, 3))

            def transpose_weights(b, groups):
                for g in groups:
                    if g < 4:
                        if not isinstance(b, int):
                            wait(pe, s_rm, NPROJ * (b + 1) + NPROJ - 3 + g)
                    else:
                        wait(pe, (s_td, s_ta)[g % 2], HG * b + g // 2 - 1)
                    q = g if g < NP // 4 else g - NP // 4 + NP // 8
                    if g < ACT_AT:
                        wait(pe, s_n, ACT_AT * b + g + 1)
                    elif g < NP // 4:
                        wait(pe, s_na, (NPAIR - ACT_AT) * b + g - ACT_AT + 1)
                    hi = 0 if g < NP // 4 else 128
                    for j in range(4):
                        last = pe.transpose(four[g % 4][:, 128 * j:128 * (j + 1)], p_slot(4 * q + j)[:, hi:hi + 128], ident[:, :])
                    last.then_inc(s_t, 1)

            def finish_attention(b, done):
                transpose_weights(b, range(4, NGRP))
                wait(pe, s_td, HG * b + NP // 8)
                wait(pe, s_ta, HG * b + NP // 8)
                wait(pe, s_v, 4 * (b + 1))
                wait(pe, s_l0, NPAIR * done)
                wait(pe, s_l1, NPAIR * done)

                def heads_output(c, tiles):
                    for t in tiles:
                        for e in range(2):
                            h, r = 2 * c + e, slice(64 * e, 64 * e + 64)
                            o = other[c % 4][r, 128 * t:L]
                            last = mm(o, V[:, t, D * h:D * (h + 1)], (PT0, PT1)[t][:, h, :], start=(t == 0), stop=(t == 1))
                    return last
                heads_output(0, [0])
                heads_output(1, [0])
                wait(pe, s_td, HG * (b + 1))
                wait(pe, s_ta, HG * (b + 1))
                for c in range(NPAIR):
                    if c >= 4:
                        wait(pe, s_o, NPAIR * b + c - 3)
                    heads_output(c, [0, 1] if c >= 2 else [1]).then_inc(s_pv, 1)
                    if c >= 2:
                        output(b, c - 2)
                output(b, NPAIR - 2)
                output(b, NPAIR - 1)

            def output(b, c):
                wait(pe, s_o, NPAIR * b + c + 1)
                for t in range(TT):
                    last = mm(bank[t][:, 0:HID], OT[:, c % 4, 128 * t:128 * (t + 1)], wo[:, c, :],
                              start=(c == 0), stop=(c == NPAIR - 1))
                last.then_inc(s_yp, 1)

            def second_transposes(b):
                wait(pe, s_xn2, b + 1)
                for t in range(TT):
                    last = pe.transpose(bank[0][:, 128 * t:128 * (t + 1)], xn[:, t, :], ident[:, :])
                last.then_inc(s_tr2, 1)

            def route(b):
                wait(pe, s_hl2, b + 1)
                for t in range(TT):
                    last = mm3(bank[1][:, E * t:E * (t + 1)], lambda j: hcur[:, j, 128 * t:128 * (t + 1)],
                               lambda j: gw[:, j, :])
                last.then_inc(s_rp, 1)

            def values_and_mlp(b, norm):
                for n in range(4):
                    if n >= 2:
                        wait(pe, s_v, 4 * b + n - 1)
                    t, q = n // 2, n % 2
                    at = 2 * H * D + 512 * q
                    mm3(bank[2 + n % 2][:, :], lambda j: hcur[:, j, 128 * t:128 * (t + 1)],
                        lambda j: wqkv[:, j, at:at + 512]).then_inc(s_vp, 1)

                def hidden(c):
                    k, m, n, w = CHUNKS[c]
                    if c == FIRST[k]:
                        wait(pe, s_x[k], 16 * 2 * PPB * (b + 1))
                    if c == 2:
                        wait(pe, s_v, 4 * (b + 1))
                    if c >= 3:
                        wait(pe, s_g, NCH * b + c - 2)
                    for par in range(2):
                        v = rows(X[k][:, par * PPB * SLOT[k]:(par + 1) * PPB * SLOT[k]], SLOT[k])[:, m:m + n, W[k] - w:W[k]]
                        o = rows(hbank[c % 3][:, par * n * w:(par + 1) * n * w], w)
                        for j in range(2):
                            last = mm(o, w1s[:, j, :], v, start=(par == 0 and j == 0), stop=(par == 1 and j == 1 and c in DVE_ADDS),
                                      skip_group_check=True)
                    t = hk[:, :, :, L - w:L]
                    for j in range(2 if c not in DVE_ADDS else 0):
                        for i in range(n):
                            o = hbank[c % 3][:, 0:2 * n * w].rearrange("p (a m t) -> p a m t", a=2, m=n)[:, :, i, :]
                            last = mm(o, identh[:, :], t[:, j, :, :], start=False, stop=(j == 1 and i == n - 1), skip_group_check=True)
                    last.then_inc(s_h, 1)

                def logits(c):
                    k, m, n, w = CHUNKS[c]
                    if c >= 2:
                        wait(pe, s_m, NCH * b + c - 1)
                    for par in range(2):
                        v = rows(X[k][:, par * PPB * SLOT[k]:(par + 1) * PPB * SLOT[k]], SLOT[k])[:, m:m + n, W[k] - w:W[k]]
                        mm(rows(bank[6 + c % 2][64 * par:64 * par + 64, 0:n * w], w), sel[:, :], v, stop=False)
                    wait(pe, s_g, NCH * b + c + 1)
                    for par in range(2):
                        last = mm(bank[6 + c % 2][64 * par:64 * par + 64, 0:n * w], w2d[:, :],
                                  Hs[:, c % 3, par * n * w:(par + 1) * n * w], start=False)
                    last.then_inc(s_l, 1)

                hidden(0)
                hidden(1)
                for c in range(NCH):
                    if c + 2 < NCH:
                        hidden(c + 2)
                    if c == 0:
                        gates_product(b)
                    logits(c)
                    if norm and c == NORM_AT:
                        second_transposes(b - 1)
                    if c == FIRST_AT:
                        first_transposes(b + 1)
                    if norm and c == ROUTE_AT:
                        route(b - 1)

            pe.wait_ge(s_wl, 2)
            pe.wait_ge(s_zero, 6)
            proj_and_scores(0, False)
            pe.wait_ge(s_l0, NPAIR)
            pe.wait_ge(s_l1, NPAIR)
            values_and_mlp(0, False)
            pe.wait_ge(s_gw, 1)
            with pe.Fori(1, B) as b:
                proj_and_scores(b, True)
                finish_attention(b - 1, b + 1)
                values_and_mlp(b, True)
            transpose_weights(B - 1, range(4))
            finish_attention(B - 1, B)
            second_transposes(B - 1)
            route(B - 1)

            pe.wait_ge(s_dr, MASK_STEPS)
            for g in range(NT // 4):
                wait(pe, s_mt, g - 6)
                for t in range(4 * g, 4 * g + 4):
                    last = pe.transpose(bank[g % 7][:, :].bitcast(bf16)[0:E, 128 * (t % 4):128 * (t % 4 + 1)], maskb[:, E * t:E * (t + 1)], identb)
                last.then_inc(s_mtp, 1)
            pe.wait_ge(s_ones, 1)
            pe.wait_ge(s_dr, ROUTER_STEPS)
            mm(bank[7][:, 0:2 * E], ones, tot[:, 0:2 * E]).then_inc(s_tp, 1)
            pe.wait_ge(s_el, 1)
            pe.wait_ge(s_mt, NT // 4)

            def down(g, u, t):
                if t == 0:
                    wait(pe, s_a2, g * 4 + 4)
                    wait(pe, s_a1, g * 5 + 5)
                    wait(pe, s_r1, g - 1)
                for m in range(5):
                    last = mm(bank[6 + u][:, HID * t:HID * (t + 1)], acts[u][:, m, 128 * t:128 * (t + 1)], dn[:, m, :],
                              start=(m == 0), stop=(m == 4))
                if t == 3:
                    last.then_inc(s_dp, 1)

            def experts(g, u):
                first = isinstance(g, int) and g == 0
                for m in range(5):
                    if m >= 2 or not first:
                        wait(pe, s_si, g * 5 + m - 1)
                    mm3(bank[(u + m) % 2][:, :], lambda j: ew[:, j, 128 * m:128 * (m + 1)], lambda j: hT[:, j, ds(g * 512, 512)]).then_inc(s_gp, 1)
                    if m >= 2 or not first:
                        wait(pe, s_a1, g * 5 + m - 1)
                    if m < 4:
                        wait(pe, s_a2, g * 4 + m - 1)
                    mm3(bank[2 + (u + m) % 2][:, :], lambda j: ew[:, j, NG + 128 * m:NG + 128 * (m + 1)], lambda j: hT[:, j, ds(g * 512, 512)]).then_inc(s_up, 1)
                    if m < 4:
                        mm(bank[4 + m % 2][:, :], pickb[:, 128 * m:128 * (m + 1)], mT[:, ds(g * 512, 512)]).then_inc(s_mb, 1)
                    if m < 4 and not first:
                        down(g - 1, 1 - u, m)
            experts(0, 0)
            pe.wait_ge(s_wm, 1)
            experts(1, 1)
            with pe.Fori(1, NT // 8) as r2:
                for u in range(2):
                    experts(r2 * 2 + u, u)
            for t in range(4):
                down(NT // 4 - 1, 1, t)


def kernel(**inputs):
    import concourse.bacc as bacc
    from concourse.bass_utils import run_bass_kernel_spmd

    v = {k.removeprefix("L0_"): np.asarray(x) for k, x in inputs.items()}
    arrays = {
        "x": v["attn_x"].reshape(B * L, HID), "wqkv": v["attn_w_qkv"], "wo": v["attn_w_o"],
        "w1": v["attn_w1"], "w2": v["attn_w2"],
        "b1": np.tile(v["attn_b1"], RI)[:, None], "b2": np.tile(v["attn_b2"], 2 * RI)[:, None],
        "pa": np.stack([np.tile(v["attn_log_p"].reshape(-1), 8), np.tile(v["attn_log_a"].reshape(-1), 8)], 1),
        "wrot": v["attn_w_qkv"][:, :2 * H * D].reshape(HID, 2 * H, 2, D // 2)[:, :, ::-1].reshape(HID, 2 * H * D),
        "cT": v["c"].T, "wmod": v["wmod"],
        "egT": v["ffn_expert_gate_w"].reshape(E * I, HID).T, "euT": v["ffn_expert_up_w"].reshape(E * I, HID).T,
        "edT": v["ffn_expert_down_w"].transpose(0, 2, 1).reshape(E * I, HID),
        "sgT": v["ffn_shared_gate_w"].T, "suT": v["ffn_shared_up_w"].T, "sdT": v["ffn_shared_down_w"].T,
        "gwT": v["ffn_gate_w"].T, "lbb": np.tile(v["ffn_lb_bias"], (128, NT)),
    }
    arrays.update(shape_constants())
    arrays = {k: np.ascontiguousarray(x) for k, x in arrays.items()}
    nc = bacc.Bacc("TRN2", target_bir_lowering=False, num_devices=1)
    a = {k: nc.dram_tensor(f"in_{k}", x.shape, mybir.dt.from_np(x.dtype), kind="ExternalInput").ap() for k, x in arrays.items()}
    out = nc.dram_tensor("out_0", (B * L, HID), mybir.dt.float32, kind="ExternalOutput").ap()
    build(nc, a, out)
    r = run_bass_kernel_spmd(nc, [{f"in_{k}": x for k, x in arrays.items()}], core_ids=[0])
    return r.results[0]["out_0"].reshape(B, L, HID)
```
